# Optimizing a Trainium2 kernel written in Bass

```python
import numpy as np
import jax
import jax.numpy as jnp

def _softmax(x, axis=-1):
    return jax.nn.softmax(x, axis=axis)

def _gelu(x):
    return jax.nn.gelu(x, approximate=True)

def _silu(x):
    return jax.nn.silu(x)

def _sigmoid(x):
    return jax.nn.sigmoid(x)

def _layernorm(x, axis=-1, eps=1e-05):
    m = jnp.mean(x, axis=axis, keepdims=True)
    v = jnp.var(x, axis=axis, keepdims=True)
    return (x - m) / jnp.sqrt(v + eps)

def _scatter_add(tgt, idx, src, axis=0):
    return tgt.at[idx].add(src)

def _segment_sum(src, seg, n):
    return jax.ops.segment_sum(src, seg, n)
kernel_name = 'mk_dlrm_tower_d1_rec_r8_7b6c91'

def setup_inputs(seed: int=0):
    np.random.seed(seed)
    _w = jnp.asarray

    def _rec_inputs():
        import jax
        import jax.numpy as jnp
        _tk = jax.random.key(seed)
        ids = jnp.stack([jax.random.randint(jax.random.fold_in(_tk, 200 + f), (512,), 0, v, jnp.int32) for f, v in enumerate([1250, 125000, 1000, 12500, 1250, 1000, 1250, 12500, 1000, 1250, 12500, 12500, 1250, 1000, 1000, 1250, 1000, 1000, 12500, 1000, 12500, 12500, 1250, 12500, 1250, 1250])], axis=1)
        tbl_0 = 0.05 * jax.random.normal(jax.random.fold_in(_tk, 500 + 0), (1250, 128), jnp.float32)
        tbl_1 = 0.05 * jax.random.normal(jax.random.fold_in(_tk, 500 + 1), (125000, 128), jnp.float32)
        tbl_2 = 0.05 * jax.random.normal(jax.random.fold_in(_tk, 500 + 2), (1000, 128), jnp.float32)
        tbl_3 = 0.05 * jax.random.normal(jax.random.fold_in(_tk, 500 + 3), (12500, 128), jnp.float32)
        tbl_4 = 0.05 * jax.random.normal(jax.random.fold_in(_tk, 500 + 4), (1250, 128), jnp.float32)
        tbl_5 = 0.05 * jax.random.normal(jax.random.fold_in(_tk, 500 + 5), (1000, 128), jnp.float32)
        tbl_6 = 0.05 * jax.random.normal(jax.random.fold_in(_tk, 500 + 6), (1250, 128), jnp.float32)
        tbl_7 = 0.05 * jax.random.normal(jax.random.fold_in(_tk, 500 + 7), (12500, 128), jnp.float32)
        tbl_8 = 0.05 * jax.random.normal(jax.random.fold_in(_tk, 500 + 8), (1000, 128), jnp.float32)
        tbl_9 = 0.05 * jax.random.normal(jax.random.fold_in(_tk, 500 + 9), (1250, 128), jnp.float32)
        tbl_10 = 0.05 * jax.random.normal(jax.random.fold_in(_tk, 500 + 10), (12500, 128), jnp.float32)
        tbl_11 = 0.05 * jax.random.normal(jax.random.fold_in(_tk, 500 + 11), (12500, 128), jnp.float32)
        tbl_12 = 0.05 * jax.random.normal(jax.random.fold_in(_tk, 500 + 12), (1250, 128), jnp.float32)
        tbl_13 = 0.05 * jax.random.normal(jax.random.fold_in(_tk, 500 + 13), (1000, 128), jnp.float32)
        tbl_14 = 0.05 * jax.random.normal(jax.random.fold_in(_tk, 500 + 14), (1000, 128), jnp.float32)
        tbl_15 = 0.05 * jax.random.normal(jax.random.fold_in(_tk, 500 + 15), (1250, 128), jnp.float32)
        tbl_16 = 0.05 * jax.random.normal(jax.random.fold_in(_tk, 500 + 16), (1000, 128), jnp.float32)
        tbl_17 = 0.05 * jax.random.normal(jax.random.fold_in(_tk, 500 + 17), (1000, 128), jnp.float32)
        tbl_18 = 0.05 * jax.random.normal(jax.random.fold_in(_tk, 500 + 18), (12500, 128), jnp.float32)
        tbl_19 = 0.05 * jax.random.normal(jax.random.fold_in(_tk, 500 + 19), (1000, 128), jnp.float32)
        tbl_20 = 0.05 * jax.random.normal(jax.random.fold_in(_tk, 500 + 20), (12500, 128), jnp.float32)
        tbl_21 = 0.05 * jax.random.normal(jax.random.fold_in(_tk, 500 + 21), (12500, 128), jnp.float32)
        tbl_22 = 0.05 * jax.random.normal(jax.random.fold_in(_tk, 500 + 22), (1250, 128), jnp.float32)
        tbl_23 = 0.05 * jax.random.normal(jax.random.fold_in(_tk, 500 + 23), (12500, 128), jnp.float32)
        tbl_24 = 0.05 * jax.random.normal(jax.random.fold_in(_tk, 500 + 24), (1250, 128), jnp.float32)
        tbl_25 = 0.05 * jax.random.normal(jax.random.fold_in(_tk, 500 + 25), (1250, 128), jnp.float32)
        _rk = jax.random.fold_in(_tk, 7)
        r_dense_features = -0.000520686 + 1.00062 * jax.random.normal(jax.random.fold_in(_rk, 101), (512, 128), jnp.float32)
        W_top1 = 0.0405887 * jax.random.normal(jax.random.fold_in(_tk, 801), (607, 512), jnp.float32)
        W_top2 = 0.0441942 * jax.random.normal(jax.random.fold_in(_tk, 802), (512, 256), jnp.float32)
        W_top3 = 0.0625 * jax.random.normal(jax.random.fold_in(_tk, 803), (256, 1), jnp.float32)
        b_top1 = jnp.zeros((512,), jnp.float32)
        b_top2 = jnp.zeros((256,), jnp.float32)
        return (r_dense_features, ids, tbl_0, tbl_1, tbl_2, tbl_3, tbl_4, tbl_5, tbl_6, tbl_7, tbl_8, tbl_9, tbl_10, tbl_11, tbl_12, tbl_13, tbl_14, tbl_15, tbl_16, tbl_17, tbl_18, tbl_19, tbl_20, tbl_21, tbl_22, tbl_23, tbl_24, tbl_25, W_top1, b_top1, W_top2, b_top2, W_top3)
    r_dense_features, ids, tbl_0, tbl_1, tbl_2, tbl_3, tbl_4, tbl_5, tbl_6, tbl_7, tbl_8, tbl_9, tbl_10, tbl_11, tbl_12, tbl_13, tbl_14, tbl_15, tbl_16, tbl_17, tbl_18, tbl_19, tbl_20, tbl_21, tbl_22, tbl_23, tbl_24, tbl_25, W_top1, b_top1, W_top2, b_top2, W_top3 = _rec_inputs()

    def _L0_rec_setup():
        import jax, jax.numpy as jnp
        import numpy as np
        B, F, D = (2048, 26, 128)
        key = jax.random.key(seed)
        k1, k2 = jax.random.split(key)
        dense_features = jax.random.normal(k1, (B, D), dtype=jnp.float32)
        sparse_values = jax.random.normal(k2, (B, F, D), dtype=jnp.float32)
        return {'dense_features': dense_features, 'sparse_values': sparse_values}
    _L0_rec_all = _L0_rec_setup()
    _L0_rec_in = {k: v for k, v in _L0_rec_all.items() if k in ()}
    del _L0_rec_all
    return {'r_dense_features': r_dense_features, 'ids': ids, 'tbl_0': tbl_0, 'tbl_1': tbl_1, 'tbl_2': tbl_2, 'tbl_3': tbl_3, 'tbl_4': tbl_4, 'tbl_5': tbl_5, 'tbl_6': tbl_6, 'tbl_7': tbl_7, 'tbl_8': tbl_8, 'tbl_9': tbl_9, 'tbl_10': tbl_10, 'tbl_11': tbl_11, 'tbl_12': tbl_12, 'tbl_13': tbl_13, 'tbl_14': tbl_14, 'tbl_15': tbl_15, 'tbl_16': tbl_16, 'tbl_17': tbl_17, 'tbl_18': tbl_18, 'tbl_19': tbl_19, 'tbl_20': tbl_20, 'tbl_21': tbl_21, 'tbl_22': tbl_22, 'tbl_23': tbl_23, 'tbl_24': tbl_24, 'tbl_25': tbl_25, 'W_top1': W_top1, 'b_top1': b_top1, 'W_top2': W_top2, 'b_top2': b_top2, 'W_top3': W_top3}

def reference(r_dense_features, ids, tbl_0, tbl_1, tbl_2, tbl_3, tbl_4, tbl_5, tbl_6, tbl_7, tbl_8, tbl_9, tbl_10, tbl_11, tbl_12, tbl_13, tbl_14, tbl_15, tbl_16, tbl_17, tbl_18, tbl_19, tbl_20, tbl_21, tbl_22, tbl_23, tbl_24, tbl_25, W_top1, b_top1, W_top2, b_top2, W_top3):
    import jax
    import jax.numpy as jnp

    def _L0_rec_ref(dense_features, sparse_values):
        import jax, jax.numpy as jnp
        import numpy as np
        B, F, D = (2048, 26, 128)
        sd = jnp.einsum('bfd,bd->bf', sparse_values, dense_features)
        ss = jnp.einsum('bfd,bgd->bfg', sparse_values, sparse_values)
        iu, ju = jnp.triu_indices(F, k=1)
        pairs = ss[:, iu, ju]
        return jnp.concatenate([dense_features, sd, pairs], axis=1)
    e = jnp.stack([tbl_0[ids[:, 0]], tbl_1[ids[:, 1]], tbl_2[ids[:, 2]], tbl_3[ids[:, 3]], tbl_4[ids[:, 4]], tbl_5[ids[:, 5]], tbl_6[ids[:, 6]], tbl_7[ids[:, 7]], tbl_8[ids[:, 8]], tbl_9[ids[:, 9]], tbl_10[ids[:, 10]], tbl_11[ids[:, 11]], tbl_12[ids[:, 12]], tbl_13[ids[:, 13]], tbl_14[ids[:, 14]], tbl_15[ids[:, 15]], tbl_16[ids[:, 16]], tbl_17[ids[:, 17]], tbl_18[ids[:, 18]], tbl_19[ids[:, 19]], tbl_20[ids[:, 20]], tbl_21[ids[:, 21]], tbl_22[ids[:, 22]], tbl_23[ids[:, 23]], tbl_24[ids[:, 24]], tbl_25[ids[:, 25]]], axis=1)
    z = _L0_rec_ref(r_dense_features, e)
    z = z.reshape(z.shape[0], -1)
    h = jnp.concatenate([z, r_dense_features], axis=1)
    h = jnp.maximum(h @ W_top1 + b_top1, 0.0)
    h = jnp.maximum(h @ W_top2 + b_top2, 0.0)
    y = h @ W_top3
    return y

_drawn_inputs = setup_inputs


def setup_inputs(seed=0):
    import zlib

    import numpy as np

    out = dict(_drawn_inputs(seed))
    spreads = {'b_top1': (0.0, 0.1), 'b_top2': (0.0, 0.1)}
    factors = {}
    for name, (base, spread) in spreads.items():
        noise = np.random.default_rng([zlib.crc32(name.encode()), seed]).standard_normal(out[name].shape)
        drawn = base * np.exp(spread * noise) if base else spread * noise
        out[name] = jnp.asarray(drawn.astype(out[name].dtype))
    for name, factor in factors.items():
        out[name] = (out[name] * factor).astype(out[name].dtype)
    return out
```

```python
import numpy as np
import concourse.bass as bass
from concourse import mybir
from contextlib import ExitStack

BATCH, FIELDS, DIM = 512, 26, 128
HID1, HID2 = 512, 256
TILE = 128
TILES = BATCH // TILE
QUAD = 4
GROUPS = TILE // QUAD
SLOT = 32
FEATS = FIELDS + 1
DENSE_SLOT = FIELDS
DIAGS = FEATS // 2
UNWRAPPED = FEATS - DIAGS
PAIRS = DIAGS * FEATS
PAIR_TILES = 3
PAIR_ROWS = PAIRS // PAIR_TILES
PER_BANK = 4
BANKS_OF_SLOTS = (FEATS + PER_BANK - 1) // PER_BANK
GRAM_COLS = QUAD * FEATS
CHUNKS = 4
CHUNK_GROUPS = GROUPS // CHUNKS


def pair_row_order():
    row_of = {}
    for f in range(FIELDS):
        row_of[(f, DENSE_SLOT)] = DIM + f
    row = DIM + FIELDS
    for f in range(FIELDS):
        for g in range(f + 1, FIELDS):
            row_of[(f, g)] = row
            row += 1
    order = []
    for k in range(1, DIAGS + 1):
        for f in range(FEATS):
            g = (f + k) % FEATS
            order.append(row_of[(min(f, g), max(f, g))])
    return np.array(order)


def dlrm_tower(nc, dense, ids, tables, w_pairs, w_dense, b1, w2, b2, w3, out):
    fp32 = mybir.dt.float32
    i32 = mybir.dt.int32
    ALU = mybir.AluOpType
    ACT = mybir.ActivationFunctionType
    J1, J2 = HID1 // 128, HID2 // 128

    ctx = ExitStack()
    with ctx:
        def sb(name, shape, dt=fp32):
            return ctx.enter_context(nc.sbuf_tensor(name, shape, dt))

        def pb(name, shape):
            return ctx.enter_context(nc.psum_tensor(name, shape, fp32))

        def sem(name):
            return ctx.enter_context(nc.semaphore(name))

        ids_sb = sb("ids_sb", [128, (TILES + 1) * FIELDS], i32)
        tile_ids = sb("tile_ids", [128, FIELDS], i32)
        rows = sb("rows", [128, FIELDS, DIM])
        dense_rows = sb("dense_rows", [128, TILES, DIM])
        dense_t = sb("dense_t", [128, BATCH])
        feats_t = sb("feats_t", [128, GROUPS, QUAD, SLOT])
        gram = sb("gram", [128, GROUPS, FEATS])
        gram_by_sample = sb("gram_by_sample", [128, FEATS + DIAGS, SLOT])
        pairs = sb("pairs", [128, DIAGS, FEATS])
        pairs_t = sb("pairs_t", [PAIR_ROWS, PAIR_TILES, TILE])
        h1_t = sb("h1_t", [128, J1, TILE])
        h2_t = sb("h2_t", [128, J2, TILE])
        y_row = sb("y_row", [1, BATCH])
        w_pairs_sb = sb("w_pairs_sb", [PAIR_ROWS, PAIR_TILES, HID1])
        w_dense2_sb = sb("w_dense2_sb", [128, 2, HID1])
        w_dense_sb = sb("w_dense_sb", [128, HID1])
        w2_sb = sb("w2_sb", [128, J1, HID2])
        w3_sb = sb("w3_sb", [128, J2])
        b1_sb = sb("b1_sb", [128, J1])
        b2_sb = sb("b2_sb", [128, J2])
        ones = sb("ones", [128, 128])
        ident = sb("ident", [128, 128])

        feats_ps = [pb(f"feats_ps{i}", [128, PER_BANK, TILE]) for i in range(2)]
        gram_ps = [pb(f"gram_ps{i}", [128, 2, 512]) for i in range(2)]
        pairs_ps = pb("pairs_ps", [128, 512])
        y_ps = pb("y_ps", [1, 512])
        h1_ps = gram_ps[0][:, :, 0:HID1 // 2].rearrange("p c (j b) -> p c j b", b=TILE)
        h2_ps = gram_ps[1][:, :, 0:HID2 // 2].rearrange("p c (j b) -> p c j b", b=TILE)
        H1, H2 = J1 // 2, J2 // 2

        ids_loaded = sem("ids_loaded")
        ids_staged = sem("ids_staged")
        dense_loaded = sem("dense_loaded")
        weights_loaded = sem("weights_loaded")
        ones_set = sem("ones_set")
        ident_set = sem("ident_set")
        padding_set = sem("padding_set")
        w_dense_summed = sem("w_dense_summed")
        dense_transposed = sem("dense_transposed")
        dense_t_copied = sem("dense_t_copied")
        gathered = [sem(f"gathered{g}") for g in range(BANKS_OF_SLOTS)]
        bank_transposed = sem("bank_transposed")
        act_bank_copied = sem("act_bank_copied")
        dve_bank_copied = sem("dve_bank_copied")
        dense_slot_filled = sem("dense_slot_filled")
        chunk_computed = sem("chunk_computed")
        act_diag_copied = sem("act_diag_copied")
        dve_diag_copied = sem("dve_diag_copied")
        gram_turned = sem("gram_turned")
        act_pairs_packed = sem("act_pairs_packed")
        dve_pairs_packed = sem("dve_pairs_packed")
        pairs_turned = sem("pairs_turned")
        pairs_copied = sem("pairs_copied")
        h1_computed = sem("h1_computed")
        act_h1_rectified = sem("act_h1_rectified")
        dve_h1_rectified = sem("dve_h1_rectified")
        h2_computed = sem("h2_computed")
        act_h2_rectified = sem("act_h2_rectified")
        dve_h2_rectified = sem("dve_h2_rectified")
        y_computed = sem("y_computed")
        y_copied = sem("y_copied")
        out_written = sem("out_written")

        def slots_of(bank):
            return range(bank * PER_BANK, min((bank + 1) * PER_BANK, FIELDS))

        ACT_BANKS = (BANKS_OF_SLOTS + 1) // 2
        DVE_BANKS = BANKS_OF_SLOTS // 2
        EARLY_BANKS = 3
        EARLY_FIELDS = EARLY_BANKS * PER_BANK
        gram_flat = gram_by_sample[:, :, :].rearrange("p g f -> p (g f)")

        pairs_flat = pairs[:, :, :].rearrange("p k f -> p (k f)")

        def pair_view(first_f, count):
            base = gram_flat[:, SLOT + (SLOT + 1) * first_f:SLOT + (SLOT + 1) * first_f + 1]
            return bass.AP(base.tensor, base.offset, [list(base.ap[0]), [SLOT, DIAGS], [SLOT + 1, count]])

        block_ctx = ctx.enter_context(nc.Block())

        @block_ctx.sync
        def _(sp):
            sp.dma_start(ids_sb[:, 0:TILES * FIELDS].rearrange("p (t f) -> p t f", t=TILES),
                         ids.rearrange("(t p) f -> p t f", p=TILE)).then_inc(ids_loaded, 16)
            sp.dma_start(dense_rows[:, :, :], dense.rearrange("(t p) d -> p t d", p=TILE)).then_inc(dense_loaded, 16)
            sp.dma_start(w_pairs_sb[:, :, :],
                         w_pairs.rearrange("(t p) n -> p t n", p=PAIR_ROWS)).then_inc(weights_loaded, 16)
            sp.dma_start(w2_sb[:, :, :], w2.rearrange("(j p) n -> p j n", p=128)).then_inc(weights_loaded, 16)
            sp.wait_ge(y_copied, TILES)
            sp.dma_start(out, y_row[:, :]).then_inc(out_written, 16)
            sp.wait_ge(out_written, 16)

        @block_ctx.gpsimd
        def _(pool):
            nc.gpsimd.memset(ones[:, :], 1.0).then_inc(ones_set, 1)
            pool.wait_ge(ones_set, 1)
            nc.gpsimd.affine_select(out=ident[:, :], in_=ones[:, :], compare_op=ALU.is_equal, fill=0.0, base=0,
                                    pattern=[[-1, 128]], channel_multiplier=1).then_inc(ident_set, 1)

            def gather_tile(t):
                for bank in range(BANKS_OF_SLOTS):
                    if bank == 0:
                        pool.wait_ge(ids_staged, t * 2 + 1)
                        pool.nop(nofuse=True)
                    if bank == EARLY_BANKS:
                        pool.wait_ge(ids_staged, t * 2 + 2)
                        pool.nop(nofuse=True)
                    for f in slots_of(bank):
                        nc.gpsimd.indirect_dma_start(
                            out=rows[:, f, :], out_offset=None, in_=tables[f],
                            in_offset=bass.IndirectOffsetOnAxis(ap=tile_ids[:, f:f + 1], axis=0),
                        ).then_inc(gathered[bank], 16)

            gather_tile(0)
            with pool.Fori(1, TILES) as t:
                gather_tile(t)

        @block_ctx.tensor
        def _(pe):
            pe.wait_ge(ident_set, 1)
            pe.wait_ge(dense_loaded, 16)
            for t in range(TILES):
                last = nc.tensor.transpose(feats_ps[0][:, t, :], dense_rows[:, t, :], ident[:, :])
            last.then_inc(dense_transposed, 1)
            pe.wait_ge(dense_t_copied, 1)
            def tensor_tile(t, first):
                for bank in range(BANKS_OF_SLOTS):
                    if bank % 2 == 0 and not (first and bank == 0):
                        pe.wait_ge(act_bank_copied, t * ACT_BANKS + bank // 2)
                    if bank % 2 == 1 and not (first and bank == 1):
                        pe.wait_ge(dve_bank_copied, t * DVE_BANKS + bank // 2)
                    pe.wait_ge(gathered[bank], (t + 1) * (16 * len(slots_of(bank))))
                    for f in slots_of(bank):
                        last = nc.tensor.transpose(feats_ps[bank % 2][:, f % PER_BANK, :], rows[:, f, :], ident[:, :])
                    last.then_inc(bank_transposed, 1)
                pe.wait_ge(act_bank_copied, (t + 1) * ACT_BANKS)
                pe.wait_ge(dve_bank_copied, (t + 1) * DVE_BANKS)
                pe.wait_ge(dense_slot_filled, t + 1)
                pe.wait_ge(padding_set, 1)
                for chunk in range(CHUNKS):
                    if chunk >= 2:
                        pe.wait_ge(act_diag_copied, t * CHUNKS + (chunk - 1))
                        pe.wait_ge(dve_diag_copied, t * CHUNKS + (chunk - 1))
                    for q in range(CHUNK_GROUPS):
                        i = chunk * CHUNK_GROUPS + q
                        bank, at = q // PER_BANK, q % PER_BANK
                        last = nc.tensor.matmul(
                            gram_ps[chunk % 2][:, bank, at * GRAM_COLS:(at + 1) * GRAM_COLS].rearrange(
                                "p (s g) -> p s g", s=QUAD),
                            feats_t[:, i, :, :].rearrange("p s f -> p (s f)"),
                            feats_t[:, i, :, 0:FEATS], start=True, stop=True)
                    last.then_inc(chunk_computed, 1)
                pe.wait_ge(act_pairs_packed, t + 1)
                pe.wait_ge(dve_pairs_packed, t + 1)
                for block in range(PAIR_TILES):
                    last = nc.tensor.transpose(pairs_ps[0:PAIR_ROWS, block * TILE:(block + 1) * TILE],
                                               pairs_flat[:, block * PAIR_ROWS:(block + 1) * PAIR_ROWS],
                                               ident[:, :])
                last.then_inc(pairs_turned, 1)
                pe.wait_ge(weights_loaded, 16 * 6)
                pe.wait_ge(w_dense_summed, 1)
                pe.wait_ge(pairs_copied, t + 1)
                for half in range(2):
                    for j in range(half * H1, (half + 1) * H1):
                        cols = slice(j * 128, (j + 1) * 128)
                        nc.tensor.matmul(h1_ps[:, half, j % H1, :], w_dense_sb[:, cols],
                                         dense_t[:, bass.ds(t * TILE, TILE)], start=True, stop=False)
                        for block in range(PAIR_TILES):
                            last = nc.tensor.matmul(h1_ps[:, half, j % H1, :], w_pairs_sb[:, block, cols],
                                                    pairs_t[:, block, :], start=False, stop=(block == PAIR_TILES - 1))
                    last.then_inc(h1_computed, 1)
                pe.wait_ge(act_h1_rectified, t + 1)
                pe.wait_ge(dve_h1_rectified, t + 1)
                for half in range(2):
                    for j in range(half * H2, (half + 1) * H2):
                        for k in range(J1):
                            last = nc.tensor.matmul(h2_ps[:, half, j % H2, :], w2_sb[:, k, j * 128:(j + 1) * 128],
                                                    h1_t[:, k, :], start=(k == 0), stop=(k == J1 - 1))
                    last.then_inc(h2_computed, 1)
                if not first:
                    pe.wait_ge(y_copied, t)
                pe.wait_ge(act_h2_rectified, t + 1)
                pe.wait_ge(dve_h2_rectified, t + 1)
                for k in range(J2):
                    last = nc.tensor.matmul(y_ps[:, 0:TILE], w3_sb[:, k:k + 1], h2_t[:, k, :],
                                            start=(k == 0), stop=(k == J2 - 1))
                last.then_inc(y_computed, 1)

            tensor_tile(0, True)
            with pe.Fori(1, TILES) as t:
                tensor_tile(t, False)

        def copy_bank(engine_copy, bank):
            n = len(slots_of(bank))
            return engine_copy(
                feats_t[:, :, :, bank * PER_BANK:bank * PER_BANK + n].rearrange("p i s q -> p s i q"),
                feats_ps[bank % 2][:, 0:n, :].rearrange("p q (s i) -> p s i q", s=QUAD))

        def copy_diagonal(engine_copy, chunk, s):
            return engine_copy(
                gram[SLOT * s:SLOT * (s + 1), chunk * CHUNK_GROUPS:(chunk + 1) * CHUNK_GROUPS, :].rearrange(
                    "p (c q) g -> p c q g", c=2),
                gram_ps[chunk % 2][SLOT * s:SLOT * (s + 1), :, 0:PER_BANK * GRAM_COLS].rearrange(
                    "p c (q s g) -> p c q s g", q=PER_BANK, s=QUAD)[:, :, :, s, :])

        @block_ctx.scalar
        def _(act):
            act.dma_start(w_dense2_sb[:, :, :], w_dense.rearrange("(c p) n -> p c n", c=2)).then_inc(weights_loaded, 16)
            with nc.allow_non_contiguous_dma(reason="bias and last-layer vectors, one value per partition"):
                act.dma_start(b1_sb[:, :], b1.rearrange("(j p) -> p j", p=128)).then_inc(weights_loaded, 16)
                act.dma_start(b2_sb[:, :], b2.rearrange("(j p) -> p j", p=128)).then_inc(weights_loaded, 16)
                act.dma_start(w3_sb[:, :], w3.rearrange("(j p) o -> p (j o)", p=128)).then_inc(weights_loaded, 16)
            act.wait_ge(dense_transposed, 1)
            nc.scalar.copy(dense_t[:, :], feats_ps[0][:, :, :].rearrange("p t b -> p (t b)")).then_inc(dense_t_copied, 1)
            def scalar_tile(t, first):
                for bank in range(0, BANKS_OF_SLOTS, 2):
                    act.wait_ge(bank_transposed, t * BANKS_OF_SLOTS + (bank + 1))
                    copy_bank(nc.scalar.copy, bank).then_inc(act_bank_copied, 1)
                if not first:
                    act.wait_ge(gram_turned, t * 2)
                for chunk in range(CHUNKS):
                    act.wait_ge(chunk_computed, t * CHUNKS + (chunk + 1))
                    copy_diagonal(nc.scalar.copy, chunk, 0)
                    copy_diagonal(nc.scalar.copy, chunk, 1).then_inc(act_diag_copied, 1)
                act.wait_ge(gram_turned, t * 2 + 1)
                if not first:
                    act.wait_ge(pairs_turned, t)
                nc.scalar.copy(pairs[:, :, 0:UNWRAPPED], pair_view(0, UNWRAPPED)).then_inc(act_pairs_packed, 1)
                act.wait_ge(weights_loaded, 16 * 6)
                act.wait_ge(h1_computed, t * 2 + 1)
                for j in range(H1):
                    last = nc.scalar.activation(h1_t[:, j, :], h1_ps[:, 0, j, :], ACT.Relu, bias=b1_sb[:, j:j + 1])
                last.then_inc(act_h1_rectified, 1)
                act.wait_ge(h2_computed, t * 2 + 1)
                for j in range(H2):
                    last = nc.scalar.activation(h2_t[:, j, :], h2_ps[:, 0, j, :], ACT.Relu, bias=b2_sb[:, j:j + 1])
                last.then_inc(act_h2_rectified, 1)
                act.wait_ge(y_computed, t + 1)
                nc.scalar.copy(y_row[:, bass.ds(t * TILE, TILE)], y_ps[:, 0:TILE]).then_inc(y_copied, 1)

            scalar_tile(0, True)
            with act.Fori(1, TILES) as t:
                scalar_tile(t, False)

        @block_ctx.vector
        def _(dve):
            nc.vector.memset(ids_sb[:, TILES * FIELDS:(TILES + 1) * FIELDS], 0)
            dve.wait_ge(ids_loaded, 16)
            nc.vector.tensor_copy(tile_ids[:, :], ids_sb[:, 0:FIELDS]).then_inc(ids_staged, 2)
            nc.vector.memset(feats_t[:, :, :, FEATS:SLOT], 0.0).then_inc(padding_set, 1)
            dve.wait_ge(weights_loaded, 16 * 6)
            nc.vector.tensor_tensor(w_dense_sb[:, :], w_dense2_sb[:, 0, :], w_dense2_sb[:, 1, :],
                                    ALU.add).then_inc(w_dense_summed, 1)
            dve.wait_ge(dense_t_copied, 1)
            def vector_tile(t, first):
                if not first:
                    dve.wait_ge(chunk_computed, t * CHUNKS)
                nc.vector.tensor_copy(feats_t[:, :, :, DENSE_SLOT].rearrange("p i s -> p s i"),
                                      dense_t[:, bass.ds(t * TILE, TILE)].rearrange("p (s i) -> p s i", s=QUAD)
                                      ).then_inc(dense_slot_filled, 1)
                for bank in range(1, BANKS_OF_SLOTS, 2):
                    dve.wait_ge(bank_transposed, t * BANKS_OF_SLOTS + (bank + 1))
                    copy_bank(nc.vector.tensor_copy, bank).then_inc(dve_bank_copied, 1)
                    if bank == EARLY_BANKS:
                        nc.vector.tensor_copy(tile_ids[:, 0:EARLY_FIELDS],
                                              ids_sb[:, bass.ds(t * FIELDS + FIELDS, EARLY_FIELDS)]
                                              ).then_inc(ids_staged, 1)
                dve.wait_ge(bank_transposed, t * BANKS_OF_SLOTS + BANKS_OF_SLOTS)
                nc.vector.tensor_copy(tile_ids[:, EARLY_FIELDS:FIELDS],
                                      ids_sb[:, bass.ds(t * FIELDS + (FIELDS + EARLY_FIELDS), FIELDS - EARLY_FIELDS)]
                                      ).then_inc(ids_staged, 1)
                if not first:
                    dve.wait_ge(gram_turned, t * 2)
                for chunk in range(CHUNKS):
                    dve.wait_ge(chunk_computed, t * CHUNKS + (chunk + 1))
                    copy_diagonal(nc.vector.tensor_copy, chunk, 2)
                    copy_diagonal(nc.vector.tensor_copy, chunk, 3).then_inc(dve_diag_copied, 1)
                dve.wait_ge(act_diag_copied, (t + 1) * CHUNKS)
                dve.wait_ge(dve_diag_copied, (t + 1) * CHUNKS)
                nc.vector.transpose(gram_by_sample[:, 0:FEATS, :],
                                    gram[:, :, :].rearrange("p i g -> p g i")).then_inc(gram_turned, 1)
                nc.vector.transpose(gram_by_sample[:, FEATS:FEATS + DIAGS, :],
                                    gram[:, :, 0:DIAGS].rearrange("p i g -> p g i")).then_inc(gram_turned, 1)
                dve.wait_ge(gram_turned, (t + 1) * 2)
                nc.vector.tensor_copy(pairs[:, :, UNWRAPPED:FEATS],
                                      pair_view(UNWRAPPED, FEATS - UNWRAPPED)).then_inc(dve_pairs_packed, 1)
                dve.wait_ge(pairs_turned, t + 1)
                nc.vector.tensor_copy(pairs_t[:, :, :].rearrange("p k b -> p (k b)"),
                                      pairs_ps[0:PAIR_ROWS, 0:PAIR_TILES * TILE]).then_inc(pairs_copied, 1)
                dve.wait_ge(h1_computed, t * 2 + 2)
                for j in range(H1):
                    last = nc.vector.tensor_scalar(h1_t[:, H1 + j, :], h1_ps[:, 1, j, :],
                                                   b1_sb[:, H1 + j:H1 + j + 1], 0.0, ALU.add, ALU.max)
                last.then_inc(dve_h1_rectified, 1)
                dve.wait_ge(h2_computed, t * 2 + 2)
                for j in range(H2):
                    last = nc.vector.tensor_scalar(h2_t[:, H2 + j, :], h2_ps[:, 1, j, :],
                                                   b2_sb[:, H2 + j:H2 + j + 1], 0.0, ALU.add, ALU.max)
                last.then_inc(dve_h2_rectified, 1)

            vector_tile(0, True)
            with dve.Fori(1, TILES) as t:
                vector_tile(t, False)


def kernel(**inputs):
    import concourse.bacc as bacc
    from concourse.bass_utils import run_bass_kernel_spmd

    w1 = np.asarray(inputs["W_top1"])
    arrays = {name: np.ascontiguousarray(inputs[name])
              for name in ["r_dense_features", "ids"] + [f"tbl_{f}" for f in range(FIELDS)]}
    arrays["w_pairs"] = np.ascontiguousarray(w1[pair_row_order()])
    arrays["w_dense"] = np.ascontiguousarray(np.concatenate([w1[:DIM], w1[-DIM:]]))
    for name in ["b_top1", "W_top2", "b_top2", "W_top3"]:
        arrays[name] = np.ascontiguousarray(inputs[name])

    nc = bacc.Bacc("TRN2", target_bir_lowering=False, num_devices=1)
    ap = {name: nc.dram_tensor("in_" + name, a.shape, mybir.dt.from_np(a.dtype), kind="ExternalInput").ap()
          for name, a in arrays.items()}
    out = nc.dram_tensor("out_y", (BATCH, 1), mybir.dt.float32, kind="ExternalOutput").ap()
    dlrm_tower(nc, ap["r_dense_features"], ap["ids"], [ap[f"tbl_{f}"] for f in range(FIELDS)], ap["w_pairs"],
               ap["w_dense"], ap["b_top1"], ap["W_top2"], ap["b_top2"], ap["W_top3"], out.rearrange("b o -> o b"))
    r = run_bass_kernel_spmd(nc, [{"in_" + name: a for name, a in arrays.items()}], core_ids=[0])
    return r.results[0]["out_y"]
```

```python
import numpy as np
import concourse.bass as bass
from concourse import mybir
from contextlib import ExitStack

BATCH, FIELDS, DIM = 512, 26, 128
HID1, HID2 = 512, 256
TABLE_ROWS = [1250, 125000, 1000, 12500, 1250, 1000, 1250, 12500, 1000, 1250, 12500, 12500, 1250,
              1000, 1000, 1250, 1000, 1000, 12500, 1000, 12500, 12500, 1250, 12500, 1250, 1250]
LOOKUPS = 8
LOOKED_UP = [f for f in range(FIELDS) if TABLE_ROWS[f] == min(TABLE_ROWS)][:LOOKUPS]
GATHERED = [f for f in range(FIELDS) if f not in LOOKED_UP]
GATHERS = len(GATHERED)
LOOKUP_CHUNKS = 8
LOOKUP_PARTS = min(TABLE_ROWS) // LOOKUP_CHUNKS
DVE_CHUNKS = 6
ACT_CHUNKS = LOOKUP_CHUNKS - DVE_CHUNKS

TILE = 128
TILES = BATCH // TILE
QUAD = 4
GROUPS = TILE // QUAD
SLOTS = 32
FEATS = FIELDS + 1
RESIDENT = 1 + LOOKUPS
DIAGS = FEATS // 2
UNWRAPPED = FEATS - DIAGS
PER_BANK = 4
ROW_BANKS = (GATHERS + PER_BANK - 1) // PER_BANK
DVE_BANKS = [bank for bank in range(ROW_BANKS) if bank % 3 == 2]
ACT_BANKS = [bank for bank in range(ROW_BANKS) if bank not in DVE_BANKS]
EARLY_BANKS = 2
LATE_BANKS = 3
PLACES = 3
TABLE_BUFFERS = 2
SPLIT_BUFFERS = 3
WARM_UP = 9
GRAM_COLS = QUAD * FEATS
CHUNKS = 4
CHUNK_GROUPS = GROUPS // CHUNKS
PAIR_TILES = 3
PAIR_ROWS = DIAGS * FEATS // PAIR_TILES


def pair_row_order():
    row_of = {}
    row = DIM + FIELDS
    for f in range(FIELDS):
        row_of[(f, FIELDS)] = DIM + f
        for g in range(f + 1, FIELDS):
            row_of[(f, g)] = row
            row += 1
    feature = GATHERED + [FIELDS] + LOOKED_UP
    return np.array([row_of[tuple(sorted((feature[f], feature[(f + k) % FEATS])))]
                     for k in range(1, DIAGS + 1) for f in range(FEATS)])


def dlrm_tower(nc, dense, ids_gathered, ids_looked_up, gathered_tables, lookup_tables, w_pairs, w_dense, b1, w2, b2,
               w3, out):
    fp32 = mybir.dt.float32
    fp32r = mybir.dt.float32r
    i32 = mybir.dt.int32
    ALU = mybir.AluOpType
    ACT = mybir.ActivationFunctionType
    J1, J2 = HID1 // 128, HID2 // 128
    H1, H2 = J1 // 2, J2 // 2

    ctx = ExitStack()
    with ctx:
        def sb(name, shape, dt=fp32):
            return ctx.enter_context(nc.sbuf_tensor(name, shape, dt))

        def pb(name, shape):
            return ctx.enter_context(nc.psum_tensor(name, shape, fp32))

        def sem(name):
            return ctx.enter_context(nc.semaphore(name))

        ids_sb = sb("ids_sb", [128, TILES * GATHERS], i32)
        rows = [sb(f"rows{place}", [128, GATHERS, DIM]) for place in range(PLACES)]
        dense_rows = sb("dense_rows", [128, TILES, DIM])
        lookup_ids = sb("lookup_ids", [128, LOOKUPS, BATCH], i32)
        row_number_i = sb("row_number_i", [128, LOOKUP_CHUNKS], i32)
        row_number = sb("row_number", [128, LOOKUP_CHUNKS])
        minus_row_number = sb("minus_row_number", [128, LOOKUP_CHUNKS])
        distance = [sb(f"distance{i}", [LOOKUP_PARTS, BATCH]) for i in range(ACT_CHUNKS)]
        table = [sb(f"table{i}", [LOOKUP_PARTS, LOOKUP_CHUNKS * DIM]) for i in range(TABLE_BUFFERS)]
        table_high = [sb(f"table_high{i}", [LOOKUP_PARTS, LOOKUP_CHUNKS * DIM], fp32r)
                      for i in range(SPLIT_BUFFERS)]
        table_low = [sb(f"table_low{i}", [LOOKUP_PARTS, LOOKUP_CHUNKS * DIM], fp32r)
                      for i in range(SPLIT_BUFFERS)]
        one_hot = [[sb(f"one_hot{i}_{c}", [LOOKUP_PARTS, BATCH], fp32r) for c in range(LOOKUP_CHUNKS)]
                   for i in range(2)]
        dense_si = sb("dense_si", [128, TILES, QUAD, GROUPS])
        resident = sb("resident", [128, RESIDENT, BATCH])
        feats = sb("feats", [128, GROUPS, QUAD, SLOTS])
        gram = sb("gram", [128, GROUPS, FEATS])
        gram_by_sample = sb("gram_by_sample", [128, FEATS + DIAGS, SLOTS])
        pairs = sb("pairs", [128, DIAGS, FEATS])
        pairs_t = sb("pairs_t", [PAIR_ROWS, PAIR_TILES, TILE])
        h1_t = sb("h1_t", [128, J1, TILE])
        h2_t = sb("h2_t", [128, J2, TILE])
        y_row = sb("y_row", [1, BATCH])
        w_pairs_sb = sb("w_pairs_sb", [PAIR_ROWS, PAIR_TILES, HID1])
        w_dense2_sb = sb("w_dense2_sb", [128, 2, HID1])
        w2_sb = sb("w2_sb", [128, J1, HID2])
        w3_sb = sb("w3_sb", [128, J2])
        b1_sb = sb("b1_sb", [128, J1])
        b2_sb = sb("b2_sb", [128, J2])
        ones = sb("ones", [128, 128])
        ident = sb("ident", [128, 128])

        feats_ps = [pb(f"feats_ps{i}", [128, PER_BANK, TILE]) for i in range(2)]
        gram_ps = [pb(f"gram_ps{i}", [128, 2, 512]) for i in range(2)]
        pairs_ps = pb("pairs_ps", [128, 2, 512])
        early_gram_ps = [gram_ps[0][:, c, :].rearrange("p (n b) -> p n b", n=PER_BANK) for c in range(2)]
        bank_ps = [feats_ps[0], feats_ps[1], early_gram_ps[0], early_gram_ps[1], feats_ps[0]]
        assert ROW_BANKS <= len(bank_ps)
        h1_ps = gram_ps[1][:, :, 0:H1 * TILE].rearrange("p c (j b) -> p c j b", b=TILE)
        h2_ps = pairs_ps[:, :, 3 * TILE:(3 + H2) * TILE].rearrange("p c (j b) -> p c j b", b=TILE)
        y_ps = feats_ps[1][0:1, 0, :]
        lookup_ps = [gram_ps[1][:, c, :] for c in range(2)]

        ids_loaded = sem("ids_loaded")
        lookup_ids_loaded = [sem(f"lookup_ids_loaded{i}") for i in range(3)]
        table_loaded = [sem(f"table_loaded{i}") for i in range(TABLE_BUFFERS)]
        row_number_i_set = sem("row_number_i_set")
        row_number_set = sem("row_number_set")
        table_high_split = sem("table_high_split")
        table_low_split = sem("table_low_split")
        dve_one_hot_set = sem("dve_one_hot_set")
        act_one_hot_set = sem("act_one_hot_set")
        distance_set = sem("distance_set")
        looked_up = sem("looked_up")
        lookup_copied = sem("lookup_copied")
        dense_loaded = sem("dense_loaded")
        weights_loaded = sem("weights_loaded")
        ones_set = sem("ones_set")
        ident_set = sem("ident_set")
        padding_set = sem("padding_set")
        w_dense_summed = sem("w_dense_summed")
        dense_transposed = sem("dense_transposed")
        dense_copied = sem("dense_copied")
        gathered = [[sem(f"gathered{place}_{bank}") for bank in range(ROW_BANKS)] for place in range(PLACES)]
        bank_transposed = sem("bank_transposed")
        act_bank_copied = sem("act_bank_copied")
        dve_bank_copied = sem("dve_bank_copied")
        resident_placed = sem("resident_placed")
        chunk_computed = sem("chunk_computed")
        act_diag_copied = sem("act_diag_copied")
        dve_diag_copied = sem("dve_diag_copied")
        gram_turned = sem("gram_turned")
        act_pairs_packed = sem("act_pairs_packed")
        dve_pairs_packed = sem("dve_pairs_packed")
        pairs_turned = sem("pairs_turned")
        act_pairs_copied = sem("act_pairs_copied")
        dve_pairs_copied = sem("dve_pairs_copied")
        h1_computed = sem("h1_computed")
        act_h1_rectified = sem("act_h1_rectified")
        dve_h1_rectified = sem("dve_h1_rectified")
        h2_computed = sem("h2_computed")
        act_h2_rectified = sem("act_h2_rectified")
        dve_h2_rectified = sem("dve_h2_rectified")
        y_computed = sem("y_computed")
        y_copied = sem("y_copied")
        out_written = sem("out_written")
        WEIGHT_LOADS = 16 * 6

        def slots_of(bank):
            return range(bank * PER_BANK, min((bank + 1) * PER_BANK, GATHERS))

        dense_si_flat = dense_si[:, :, :, :].rearrange("p t s i -> p (t s i)")

        def tile_columns(t):
            return bass.ds(t * TILE, TILE)

        def by_slot(first, count):
            return feats[:, :, :, first:first + count].rearrange("p i s n -> p n (i s)")

        def copy_bank(engine_copy, bank):
            n = len(slots_of(bank))
            return engine_copy(by_slot(bank * PER_BANK, n), bank_ps[bank][:, 0:n, :])

        pairs_flat = pairs[:, :, :].rearrange("p k f -> p (k f)")

        def pair_view(first_f, count):
            base = gram_by_sample[:, 1 + first_f, first_f:first_f + 1]
            return bass.AP(base.tensor, base.offset, [list(base.ap[0]), [SLOTS, DIAGS], [SLOTS + 1, count]])

        def load_lookup_ids(engine, first, end, loaded):
            engine.dma_start(lookup_ids[:, first:end, :].rearrange("p n b -> p (n b)"),
                             ids_looked_up[first * BATCH:end * BATCH].partition_broadcast(128)).then_inc(loaded, 16)

        block = ctx.enter_context(nc.Block())

        @block.sync
        def _(sp):
            sp.dma_start(ids_sb[:, 0:TILES * GATHERS].rearrange("p (t f) -> p t f", t=TILES),
                         ids_gathered.rearrange("(t p) f -> p t f", p=TILE)).then_inc(ids_loaded, 16)
            def load_table(j):
                rows_first = 112 * LOOKUP_CHUNKS
                sp.dma_start(table[j % TABLE_BUFFERS][0:112, :],
                             lookup_tables[j][0:rows_first, :].rearrange("(p c) d -> p (c d)", c=LOOKUP_CHUNKS)
                             ).then_inc(table_loaded[j % TABLE_BUFFERS], 16)
                sp.dma_start(table[j % TABLE_BUFFERS][112:LOOKUP_PARTS, :],
                             lookup_tables[j][rows_first:, :].rearrange("(p c) d -> p (c d)", c=LOOKUP_CHUNKS)
                             ).then_inc(table_loaded[j % TABLE_BUFFERS], 16)

            load_table(0)
            sp.dma_start(dense_rows[:, :, :], dense.rearrange("(t p) d -> p t d", p=TILE)).then_inc(dense_loaded, 16)
            load_lookup_ids(sp, 1, 2, lookup_ids_loaded[1])
            load_table(1)
            load_lookup_ids(sp, 2, LOOKUPS, lookup_ids_loaded[2])
            for j in range(TABLE_BUFFERS, LOOKUPS):
                sp.wait_ge(table_low_split, j - TABLE_BUFFERS + 1)
                load_table(j)
            sp.dma_start(w_pairs_sb[:, :, :],
                         w_pairs.rearrange("(t p) n -> p t n", p=PAIR_ROWS)).then_inc(weights_loaded, 16)
            sp.dma_start(w2_sb[:, :, :], w2.rearrange("(j p) n -> p j n", p=128)).then_inc(weights_loaded, 16)
            sp.dma_start(w_dense2_sb[:, :, :], w_dense.rearrange("(c p) n -> p c n", c=2)).then_inc(weights_loaded, 16)
            with nc.allow_non_contiguous_dma(reason="bias and last-layer vectors, one value per partition"):
                sp.dma_start(b1_sb[:, :], b1.rearrange("(j p) -> p j", p=128)).then_inc(weights_loaded, 16)
                sp.dma_start(b2_sb[:, :], b2.rearrange("(j p) -> p j", p=128)).then_inc(weights_loaded, 16)
                sp.dma_start(w3_sb[:, :], w3.rearrange("(j p) o -> p (j o)", p=128)).then_inc(weights_loaded, 16)
            sp.wait_ge(y_copied, TILES)
            sp.dma_start(out, y_row[:, :]).then_inc(out_written, 16)
            sp.wait_ge(out_written, 16)

        @block.gpsimd
        def _(pool):
            nc.gpsimd.iota(row_number_i[:, :], pattern=[[1, LOOKUP_CHUNKS]], base=0,
                           channel_multiplier=LOOKUP_CHUNKS).then_inc(row_number_i_set, 1)
            nc.gpsimd.memset(ones[:, :], 1.0).then_inc(ones_set, 1)
            pool.wait_ge(ones_set, 1)
            nc.gpsimd.affine_select(out=ident[:, :], in_=ones[:, :], compare_op=ALU.is_equal, fill=0.0, base=0,
                                    pattern=[[-1, 128]], channel_multiplier=1).then_inc(ident_set, 1)

            pool.wait_ge(ids_loaded, 16)
            for t in range(TILES):
                place = min(t, PLACES - 1)
                for bank in range(ROW_BANKS):
                    if t >= PLACES:
                        pool.wait_ge(bank_transposed, (t - 1) * ROW_BANKS + bank + 1)
                        pool.nop(nofuse=True)
                    for slot in slots_of(bank):
                        ids_column = t * GATHERS + slot
                        nc.gpsimd.indirect_dma_start(
                            out=rows[place][:, slot, :], out_offset=None, in_=gathered_tables[slot],
                            in_offset=bass.IndirectOffsetOnAxis(ap=ids_sb[:, ids_column:ids_column + 1], axis=0),
                        ).then_inc(gathered[place][bank], 16)

        @block.tensor
        def _(pe):
            def look_up(j):
                if j >= 2:
                    pe.wait_ge(lookup_copied, j - 1)
                pe.wait_ge(table_high_split, j + 1)
                for c in range(LOOKUP_CHUNKS):
                    if c < DVE_CHUNKS:
                        pe.wait_ge(dve_one_hot_set, j * DVE_CHUNKS + c + 1)
                    else:
                        pe.wait_ge(act_one_hot_set, j * ACT_CHUNKS + c - DVE_CHUNKS + 1)
                    nc.tensor.matmul(lookup_ps[j % 2], table_high[j % SPLIT_BUFFERS][:, c * DIM:(c + 1) * DIM],
                                     one_hot[j % 2][c][:, :], start=(c == 0), stop=False)
                pe.wait_ge(table_low_split, j + 1)
                for c in range(LOOKUP_CHUNKS):
                    last = nc.tensor.matmul(lookup_ps[j % 2], table_low[j % SPLIT_BUFFERS][:, c * DIM:(c + 1) * DIM],
                                            one_hot[j % 2][c][:, :], start=False, stop=(c == LOOKUP_CHUNKS - 1))
                last.then_inc(looked_up, 1)

            def transpose_bank(t, place, bank):
                if bank in (2, 3) and place > 0:
                    pe.wait_ge(act_diag_copied, t * CHUNKS - 1)
                    pe.wait_ge(dve_diag_copied, t * CHUNKS - 1)
                if bank >= 4:
                    pe.wait_ge(act_bank_copied, t * len(ACT_BANKS) + (ACT_BANKS.index(bank - 4) + 1))
                tiles_here = t - (PLACES - 2) if place == PLACES - 1 else 1
                pe.wait_ge(gathered[place][bank], tiles_here * (16 * len(slots_of(bank))))
                for slot in slots_of(bank):
                    last = nc.tensor.transpose(bank_ps[bank][:, slot % PER_BANK, :], rows[place][:, slot, :],
                                               ident[:, :])
                last.then_inc(bank_transposed, 1)

            def second_layer(t):
                pe.wait_ge(act_h1_rectified, t + 1)
                for k in range(J1):
                    if k == H1:
                        pe.wait_ge(dve_h1_rectified, t + 1)
                    for j in range(J2):
                        last = nc.tensor.matmul(h2_ps[:, j // H2, j % H2, :], w2_sb[:, k, j * 128:(j + 1) * 128],
                                                h1_t[:, k, :], start=(k == 0), stop=(k == J1 - 1))
                        if k == J1 - 1 and j % H2 == H2 - 1:
                            last.then_inc(h2_computed, 1)

            def third_layer(t):
                for k in range(J2):
                    if k == 0:
                        pe.wait_ge(act_h2_rectified, t + 1)
                    if k == H2:
                        pe.wait_ge(dve_h2_rectified, t + 1)
                    last = nc.tensor.matmul(y_ps, w3_sb[:, k:k + 1], h2_t[:, k, :], start=(k == 0), stop=(k == J2 - 1))
                last.then_inc(y_computed, 1)

            def interact_and_classify(t, led, followed):
                pe.wait_ge(act_bank_copied, t * len(ACT_BANKS) + len(ACT_BANKS))
                pe.wait_ge(dve_bank_copied, t * len(DVE_BANKS) + len(DVE_BANKS))
                pe.wait_ge(resident_placed, t + 1)
                for chunk in range(CHUNKS):
                    if chunk == 1 and led:
                        pe.wait_ge(act_h1_rectified, t)
                        pe.wait_ge(dve_h1_rectified, t)
                    if chunk >= 2:
                        pe.wait_ge(act_diag_copied, t * CHUNKS + (chunk - 1))
                        pe.wait_ge(dve_diag_copied, t * CHUNKS + (chunk - 1))
                    for q in range(CHUNK_GROUPS):
                        i = chunk * CHUNK_GROUPS + q
                        bank, at = q // PER_BANK, q % PER_BANK
                        last = nc.tensor.matmul(
                            gram_ps[chunk % 2][:, bank, at * GRAM_COLS:(at + 1) * GRAM_COLS].rearrange(
                                "p (s g) -> p s g", s=QUAD),
                            feats[:, i, :, :].rearrange("p s f -> p (s f)"),
                            feats[:, i, :, 0:FEATS], start=True, stop=True)
                    last.then_inc(chunk_computed, 1)
                if followed:
                    for bank in range(EARLY_BANKS):
                        transpose_bank(t + 1, 2 if led else 1, bank)
                if led:
                    second_layer(t - 1)
                pe.wait_ge(weights_loaded, WEIGHT_LOADS)
                pe.wait_ge(w_dense_summed, 1)
                pe.wait_ge(act_diag_copied, t * CHUNKS + CHUNKS)
                pe.wait_ge(dve_diag_copied, t * CHUNKS + CHUNKS)
                for j in range(J1):
                    nc.tensor.matmul(h1_ps[:, j // H1, j % H1, :], w_dense2_sb[:, 0, j * 128:(j + 1) * 128],
                                     dense_si_flat[:, tile_columns(t)], start=(j % H1 == 0), stop=False,
                                     skip_group_check=True)
                if led:
                    pe.wait_ge(act_h2_rectified, t)
                    pe.wait_ge(dve_h2_rectified, t)
                pe.wait_ge(act_pairs_packed, t + 1)
                pe.wait_ge(dve_pairs_packed, t + 1)
                for k in range(PAIR_TILES):
                    last = nc.tensor.transpose(pairs_ps[0:PAIR_ROWS, k // 2, (k % 2) * TILE:(k % 2 + 1) * TILE],
                                               pairs_flat[:, k * PAIR_ROWS:(k + 1) * PAIR_ROWS], ident[:, :])
                    if k % 2 == 1 or k == PAIR_TILES - 1:
                        last.then_inc(pairs_turned, 1)
                if led:
                    if followed:
                        pe.wait_ge(act_bank_copied, (t + 1) * len(ACT_BANKS) + (ACT_BANKS.index(1) + 1))
                    third_layer(t - 1)
                if followed:
                    for bank in range(EARLY_BANKS, LATE_BANKS):
                        transpose_bank(t + 1, 2 if led else 1, bank)
                pe.wait_ge(act_pairs_copied, t + 1)
                for half in range(2):
                    for k in range(PAIR_TILES):
                        if k == PAIR_TILES - 1 and half == 0:
                            pe.wait_ge(dve_pairs_copied, t + 1)
                        for j in range(half * H1, (half + 1) * H1):
                            last = nc.tensor.matmul(h1_ps[:, half, j % H1, :],
                                                    w_pairs_sb[:, k, j * 128:(j + 1) * 128], pairs_t[:, k, :],
                                                    start=False, stop=(k == PAIR_TILES - 1), skip_group_check=True)
                    last.then_inc(h1_computed, 1)
                    if half == 0 and followed:
                        for bank in range(LATE_BANKS, ROW_BANKS):
                            transpose_bank(t + 1, 2 if led else 1, bank)

            pe.wait_ge(ones_set, 1)
            for _ in range(WARM_UP):
                nc.tensor.matmul(y_ps, ones[:, 0:1], ones[:, :], start=True, stop=True)
            pe.wait_ge(ident_set, 1)
            pe.wait_ge(dense_loaded, 16)
            for t in range(TILES):
                last = nc.tensor.transpose(pairs_ps[:, 0, t * TILE:(t + 1) * TILE], dense_rows[:, t, :], ident[:, :])
            last.then_inc(dense_transposed, 1)
            for j in range(LOOKUPS):
                look_up(j)
                if j < ROW_BANKS:
                    transpose_bank(0, 0, j)
            for bank in range(LOOKUPS, ROW_BANKS):
                transpose_bank(0, 0, bank)
            pe.wait_ge(lookup_copied, LOOKUPS)
            pe.wait_ge(dense_copied, 1)
            interact_and_classify(0, False, True)
            with pe.Fori(1, TILES - 1) as t:
                interact_and_classify(t, True, True)
            interact_and_classify(TILES - 1, True, False)
            second_layer(TILES - 1)
            third_layer(TILES - 1)

        def copy_diagonal(engine_copy, chunk, s):
            return engine_copy(
                gram[SLOTS * s:SLOTS * (s + 1), chunk * CHUNK_GROUPS:(chunk + 1) * CHUNK_GROUPS, :].rearrange(
                    "p (c q) g -> p c q g", c=2),
                gram_ps[chunk % 2][SLOTS * s:SLOTS * (s + 1), :, 0:PER_BANK * GRAM_COLS].rearrange(
                    "p c (q s g) -> p c q s g", q=PER_BANK, s=QUAD)[:, :, :, s, :])

        ACT_SAMPLES = 2

        @block.scalar
        def _(act):
            def split_table_high(j):
                act.wait_ge(table_loaded[j % TABLE_BUFFERS], (j // TABLE_BUFFERS + 1) * 32)
                if j >= SPLIT_BUFFERS:
                    act.wait_ge(looked_up, j - SPLIT_BUFFERS + 1)
                nc.scalar.copy(table_high[j % SPLIT_BUFFERS][:, :], table[j % TABLE_BUFFERS][:, :]
                               ).then_inc(table_high_split, 1)

            def copy_lookup(j):
                act.wait_ge(looked_up, j + 1)
                if j == LOOKUPS - 1:
                    act.wait_ge(resident_placed, 1)
                nc.scalar.copy(resident[:, 1 + j, :], lookup_ps[j % 2]).then_inc(lookup_copied, 1)

            def copy_transposed_bank(t, bank):
                act.wait_ge(bank_transposed, t * ROW_BANKS + (bank + 1))
                copy_bank(nc.scalar.copy, bank).then_inc(act_bank_copied, 1)

            def set_one_hot(j):
                if j == 0:
                    act.wait_ge(row_number_set, 1)
                act.wait_ge(lookup_ids_loaded[min(j, 2)], 16)
                if j >= 2:
                    act.wait_ge(looked_up, j - 1)
                if j > 0:
                    act.wait_ge(act_one_hot_set, j * ACT_CHUNKS)
                for n in range(ACT_CHUNKS):
                    c = DVE_CHUNKS + n
                    nc.scalar.activation(distance[n][:, :], lookup_ids[0:LOOKUP_PARTS, j, :], ACT.Abs,
                                         bias=minus_row_number[0:LOOKUP_PARTS, c:c + 1]).then_inc(distance_set, 1)
                for n in range(ACT_CHUNKS):
                    act.wait_ge(distance_set, j * ACT_CHUNKS + n + 1)
                    nc.scalar.activation(one_hot[j % 2][DVE_CHUNKS + n][:, :], distance[n][:, :], ACT.Relu, bias=1.0,
                                         scale=-1.0).then_inc(act_one_hot_set, 1)

            def rectify_second_layer(t):
                act.wait_ge(h2_computed, t * 2 + 1)
                for j in range(H2):
                    last = nc.scalar.activation(h2_t[:, j, :], h2_ps[:, 0, j, :], ACT.Relu, bias=b2_sb[:, j:j + 1])
                last.then_inc(act_h2_rectified, 1)

            def copy_result(t):
                act.wait_ge(y_computed, t + 1)
                nc.scalar.copy(y_row[:, tile_columns(t)].rearrange("p (i s) -> p s i", s=QUAD),
                               y_ps.rearrange("p (s i) -> p s i", s=QUAD)).then_inc(y_copied, 1)

            def interact_and_classify(t, led, followed):
                for chunk in range(CHUNKS):
                    act.wait_ge(chunk_computed, t * CHUNKS + (chunk + 1))
                    for s in range(ACT_SAMPLES):
                        last = copy_diagonal(nc.scalar.copy, chunk, s)
                    last.then_inc(act_diag_copied, 1)
                if followed:
                    for bank in range(EARLY_BANKS):
                        copy_transposed_bank(t + 1, bank)
                act.wait_ge(gram_turned, t * 2 + 1)
                nc.scalar.copy(pairs[:, :, 0:UNWRAPPED], pair_view(0, UNWRAPPED)).then_inc(act_pairs_packed, 1)
                if led:
                    rectify_second_layer(t - 1)
                act.wait_ge(pairs_turned, t * 2 + 1)
                nc.scalar.copy(pairs_t[:, 0:2, :].rearrange("p k b -> p (k b)"),
                               pairs_ps[0:PAIR_ROWS, 0, 0:2 * TILE]).then_inc(act_pairs_copied, 1)
                if led:
                    copy_result(t - 1)
                act.wait_ge(weights_loaded, WEIGHT_LOADS)
                act.wait_ge(h1_computed, t * 2 + 1)
                for j in range(H1):
                    last = nc.scalar.activation(h1_t[:, j, :], h1_ps[:, 0, j, :], ACT.Relu, bias=b1_sb[:, j:j + 1])
                last.then_inc(act_h1_rectified, 1)
                if followed:
                    for bank in ACT_BANKS[EARLY_BANKS:]:
                        copy_transposed_bank(t + 1, bank)

            load_lookup_ids(act, 0, 1, lookup_ids_loaded[0])
            split_table_high(0)
            set_one_hot(0)
            act.wait_ge(dense_transposed, 1)
            nc.scalar.copy(resident[:, 0, :], pairs_ps[:, 0, :])
            nc.scalar.copy(dense_si[:, :, :, :], pairs_ps[:, 0, :].rearrange("p (t i s) -> p t s i", t=TILES, s=QUAD)
                           ).then_inc(dense_copied, 1)
            split_table_high(1)
            for j in range(LOOKUPS):
                if j + 1 < LOOKUPS:
                    set_one_hot(j + 1)
                if j + 2 < LOOKUPS:
                    split_table_high(j + 2)
                copy_lookup(j)
                if j in ACT_BANKS:
                    copy_transposed_bank(0, j)
            interact_and_classify(0, False, True)
            with act.Fori(1, TILES - 1) as t:
                interact_and_classify(t, True, True)
            interact_and_classify(TILES - 1, True, False)
            rectify_second_layer(TILES - 1)
            copy_result(TILES - 1)

        @block.vector
        def _(dve):
            def set_one_hot(j):
                dve.wait_ge(lookup_ids_loaded[min(j, 2)], 16)
                if j >= 2:
                    dve.wait_ge(looked_up, j - 1)
                for c in range(DVE_CHUNKS):
                    nc.vector.tensor_scalar(one_hot[j % 2][c][:, :], lookup_ids[0:LOOKUP_PARTS, j, :],
                                            row_number[0:LOOKUP_PARTS, c:c + 1], None,
                                            ALU.is_equal).then_inc(dve_one_hot_set, 1)

            def split_table_low(j):
                dve.wait_ge(table_high_split, j + 1)
                nc.vector.tensor_tensor(table_low[j % SPLIT_BUFFERS][:, :], table[j % TABLE_BUFFERS][:, :],
                                        table_high[j % SPLIT_BUFFERS][:, :], ALU.subtract).then_inc(table_low_split, 1)

            def copy_transposed_bank(t, bank):
                dve.wait_ge(bank_transposed, t * ROW_BANKS + (bank + 1))
                copy_bank(nc.vector.tensor_copy, bank).then_inc(dve_bank_copied, 1)

            def place_resident(t):
                nc.vector.tensor_copy(by_slot(GATHERS, RESIDENT),
                                      resident[:, :, tile_columns(t)]).then_inc(resident_placed, 1)

            def rectify_second_layer(t):
                dve.wait_ge(h2_computed, t * 2 + 2)
                for j in range(H2, J2):
                    last = nc.vector.tensor_scalar(h2_t[:, j, :], h2_ps[:, 1, j - H2, :], b2_sb[:, j:j + 1], 0.0,
                                                   ALU.add, ALU.max)
                last.then_inc(dve_h2_rectified, 1)

            def interact_and_classify(t, led, followed):
                for chunk in range(CHUNKS):
                    dve.wait_ge(chunk_computed, t * CHUNKS + (chunk + 1))
                    for s in range(ACT_SAMPLES, QUAD):
                        last = copy_diagonal(nc.vector.tensor_copy, chunk, s)
                    last.then_inc(dve_diag_copied, 1)
                dve.wait_ge(act_diag_copied, (t + 1) * CHUNKS)
                dve.wait_ge(dve_diag_copied, (t + 1) * CHUNKS)
                nc.vector.transpose(gram_by_sample[:, 0:FEATS, :],
                                    gram[:, :, :].rearrange("p i g -> p g i")).then_inc(gram_turned, 1)
                nc.vector.transpose(gram_by_sample[:, FEATS:FEATS + DIAGS, :],
                                    gram[:, :, 0:DIAGS].rearrange("p i g -> p g i")).then_inc(gram_turned, 1)
                dve.wait_ge(gram_turned, t * 2 + 2)
                nc.vector.tensor_copy(pairs[:, :, UNWRAPPED:FEATS],
                                      pair_view(UNWRAPPED, FEATS - UNWRAPPED)).then_inc(dve_pairs_packed, 1)
                if led:
                    rectify_second_layer(t - 1)
                dve.wait_ge(pairs_turned, t * 2 + 2)
                nc.vector.tensor_copy(pairs_t[:, 2, :], pairs_ps[0:PAIR_ROWS, 1, 0:TILE]).then_inc(dve_pairs_copied, 1)
                if followed:
                    place_resident(t + 1)
                    for bank in DVE_BANKS:
                        copy_transposed_bank(t + 1, bank)
                dve.wait_ge(h1_computed, t * 2 + 2)
                for j in range(H1, J1):
                    last = nc.vector.tensor_scalar(h1_t[:, j, :], h1_ps[:, 1, j - H1, :], b1_sb[:, j:j + 1], 0.0,
                                                   ALU.add, ALU.max)
                last.then_inc(dve_h1_rectified, 1)

            nc.vector.memset(feats[:, :, :, FEATS:SLOTS], 0.0).then_inc(padding_set, 1)
            dve.wait_ge(row_number_i_set, 1)
            nc.vector.tensor_copy(row_number[:, :], row_number_i[:, :])
            nc.vector.tensor_scalar(minus_row_number[:, :], row_number_i[:, :], -1.0, None,
                                    ALU.mult).then_inc(row_number_set, 1)
            dve.wait_ge(row_number_set, 1)
            set_one_hot(0)
            split_table_low(0)
            for j in range(LOOKUPS):
                if j + 1 < LOOKUPS:
                    set_one_hot(j + 1)
                    split_table_low(j + 1)
                if j in DVE_BANKS:
                    copy_transposed_bank(0, j)
            dve.wait_ge(dense_copied, 1)
            dve.wait_ge(lookup_copied, LOOKUPS - 1)
            nc.vector.tensor_copy(by_slot(GATHERS, RESIDENT - 1), resident[:, 0:RESIDENT - 1, 0:TILE])
            dve.wait_ge(looked_up, LOOKUPS)
            nc.vector.tensor_copy(by_slot(GATHERS + RESIDENT - 1, 1), lookup_ps[(LOOKUPS - 1) % 2][:, 0:TILE]
                                  ).then_inc(resident_placed, 1)
            dve.wait_ge(lookup_copied, LOOKUPS)
            dve.wait_ge(weights_loaded, WEIGHT_LOADS)
            nc.vector.tensor_tensor(w_dense2_sb[:, 0, :], w_dense2_sb[:, 0, :], w_dense2_sb[:, 1, :],
                                    ALU.add).then_inc(w_dense_summed, 1)
            interact_and_classify(0, False, True)
            with dve.Fori(1, TILES - 1) as t:
                interact_and_classify(t, True, True)
            interact_and_classify(TILES - 1, True, False)
            rectify_second_layer(TILES - 1)


def kernel(**inputs):
    import concourse.bacc as bacc
    from concourse.bass_utils import run_bass_kernel_spmd

    ids = np.asarray(inputs["ids"])
    w1 = np.asarray(inputs["W_top1"])
    arrays = {
        "dense": np.ascontiguousarray(inputs["r_dense_features"]),
        "ids_gathered": np.ascontiguousarray(ids[:, GATHERED]),
        "ids_looked_up": np.ascontiguousarray(ids[:, LOOKED_UP].T.reshape(-1)),
        "w_pairs": np.ascontiguousarray(w1[pair_row_order()]),
        "w_dense": np.ascontiguousarray(np.concatenate([w1[:DIM], w1[-DIM:]])),
    }
    tables = [f"tbl_{f}" for f in range(FIELDS)]
    for name in tables + ["b_top1", "W_top2", "b_top2", "W_top3"]:
        arrays[name] = np.ascontiguousarray(inputs[name])

    nc = bacc.Bacc("TRN2", target_bir_lowering=False, num_devices=1)
    ap = {name: nc.dram_tensor("in_" + name, a.shape, mybir.dt.from_np(a.dtype), kind="ExternalInput").ap()
          for name, a in arrays.items()}
    out = nc.dram_tensor("out_y", (BATCH, 1), mybir.dt.float32, kind="ExternalOutput").ap()
    dlrm_tower(nc, ap["dense"], ap["ids_gathered"], ap["ids_looked_up"], [ap[tables[f]] for f in GATHERED],
               [ap[tables[f]] for f in LOOKED_UP], ap["w_pairs"], ap["w_dense"], ap["b_top1"], ap["W_top2"],
               ap["b_top2"], ap["W_top3"], out.rearrange("b o -> o b"))
    r = run_bass_kernel_spmd(nc, [{"in_" + name: a for name, a in arrays.items()}], core_ids=[0])
    return r.results[0]["out_y"]
```

```python
import numpy as np
import concourse.bass as bass
from concourse import mybir
from contextlib import ExitStack

BATCH, FIELDS, DIM = 512, 26, 128
HID1, HID2 = 512, 256
TABLE_ROWS = [1250, 125000, 1000, 12500, 1250, 1000, 1250, 12500, 1000, 1250, 12500, 12500, 1250,
              1000, 1000, 1250, 1000, 1000, 12500, 1000, 12500, 12500, 1250, 12500, 1250, 1250]
LOOKUPS = 8
LOOKED_UP = [f for f in range(FIELDS) if TABLE_ROWS[f] == min(TABLE_ROWS)][:LOOKUPS]
GATHERED = [f for f in range(FIELDS) if f not in LOOKED_UP]
GATHERS = len(GATHERED)
LOOKUP_CHUNKS = 8
LOOKUP_PARTS = min(TABLE_ROWS) // LOOKUP_CHUNKS
DVE_CHUNKS = [7 if j % 2 else 6 for j in range(LOOKUPS)]
ACT_CHUNKS = [LOOKUP_CHUNKS - chunks for chunks in DVE_CHUNKS]
DVE_CHUNKS_BEFORE = [sum(DVE_CHUNKS[:j]) for j in range(LOOKUPS)]
ACT_CHUNKS_BEFORE = [sum(ACT_CHUNKS[:j]) for j in range(LOOKUPS)]

TILE = 128
TILES = BATCH // TILE
QUAD = 4
GROUPS = TILE // QUAD
SLOTS = 32
FEATS = FIELDS + 1
RESIDENT = 1 + LOOKUPS
DIAGS = FEATS // 2
UNWRAPPED = FEATS - DIAGS
PER_BANK = 4
ROW_BANKS = (GATHERS + PER_BANK - 1) // PER_BANK
DVE_BANKS = [bank for bank in range(ROW_BANKS) if bank % 3 == 2]
ACT_BANKS = [bank for bank in range(ROW_BANKS) if bank not in DVE_BANKS]
EARLY_BANKS = 2
LATE_BANKS = 3
PLACES = 3
TABLE_BUFFERS = 2
SPLIT_BUFFERS = 3
WARM_UP = 13
GRAM_COLS = QUAD * FEATS
GRAM_ROWS = (QUAD - 1) * SLOTS + FEATS
CHUNK_BANKS = [range(0, 2), range(2, 4), range(4, 6), range(6, 7), range(7, 8)]
CHUNKS = len(CHUNK_BANKS)
assert CHUNK_BANKS[-1][-1] + 1 == GROUPS // PER_BANK
PAIR_TILES = 3
PAIR_ROWS = DIAGS * FEATS // PAIR_TILES


def pair_row_order():
    row_of = {}
    row = DIM + FIELDS
    for f in range(FIELDS):
        row_of[(f, FIELDS)] = DIM + f
        for g in range(f + 1, FIELDS):
            row_of[(f, g)] = row
            row += 1
    feature = GATHERED + [FIELDS] + LOOKED_UP
    return np.array([row_of[tuple(sorted((feature[f], feature[(f + k) % FEATS])))]
                     for k in range(1, DIAGS + 1) for f in range(FEATS)])


def dlrm_tower(nc, dense, ids_gathered, ids_looked_up, gathered_tables, lookup_tables, w_pairs, w_dense, b1, w2, b2,
               w3, out):
    fp32 = mybir.dt.float32
    fp32r = mybir.dt.float32r
    i32 = mybir.dt.int32
    ALU = mybir.AluOpType
    ACT = mybir.ActivationFunctionType
    J1 = HID1 // 128
    H1 = J1 // 2

    ctx = ExitStack()
    with ctx:
        def sb(name, shape, dt=fp32):
            return ctx.enter_context(nc.sbuf_tensor(name, shape, dt))

        def pb(name, shape):
            return ctx.enter_context(nc.psum_tensor(name, shape, fp32))

        def sem(name):
            return ctx.enter_context(nc.semaphore(name))

        ids_sb = sb("ids_sb", [128, TILES * GATHERS], i32)
        rows = [sb(f"rows{place}", [128, GATHERS, DIM]) for place in range(PLACES)]
        dense_rows = sb("dense_rows", [128, TILES, DIM])
        lookup_ids = sb("lookup_ids", [128, LOOKUPS, BATCH], i32)
        row_number_i = sb("row_number_i", [128, LOOKUP_CHUNKS], i32)
        row_number = sb("row_number", [128, LOOKUP_CHUNKS])
        minus_row_number = sb("minus_row_number", [128, LOOKUP_CHUNKS])
        distance = [sb(f"distance{i}", [LOOKUP_PARTS, BATCH]) for i in range(max(ACT_CHUNKS))]
        table = [sb(f"table{i}", [LOOKUP_PARTS, LOOKUP_CHUNKS * DIM]) for i in range(TABLE_BUFFERS)]
        table_high = [sb(f"table_high{i}", [LOOKUP_PARTS, LOOKUP_CHUNKS * DIM], fp32r)
                      for i in range(SPLIT_BUFFERS)]
        table_low = [sb(f"table_low{i}", [LOOKUP_PARTS, LOOKUP_CHUNKS * DIM], fp32r)
                      for i in range(SPLIT_BUFFERS)]
        one_hot = [[sb(f"one_hot{i}_{c}", [LOOKUP_PARTS, BATCH], fp32r) for c in range(LOOKUP_CHUNKS)]
                   for i in range(2)]
        resident = sb("resident", [128, RESIDENT, BATCH])
        feats = sb("feats", [128, GROUPS, QUAD, SLOTS])
        gram = sb("gram", [128, GROUPS, FEATS])
        gram_by_sample = sb("gram_by_sample", [128, FEATS + DIAGS, SLOTS])
        pairs = sb("pairs", [128, DIAGS, FEATS])
        pairs_t = sb("pairs_t", [PAIR_ROWS, PAIR_TILES, TILE])
        h1_t = sb("h1_t", [128, J1, TILE])
        weighted = sb("weighted", [128, HID2])
        y = sb("y", [128, TILES])
        w_pairs_sb = sb("w_pairs_sb", [PAIR_ROWS, PAIR_TILES, HID1])
        w_dense2_sb = sb("w_dense2_sb", [128, 2, HID1])
        w2_sb = sb("w2_sb", [128, J1, HID2])
        w3_sb = sb("w3_sb", [128, HID2])
        b1_sb = sb("b1_sb", [128, J1])
        b2_sb = sb("b2_sb", [1, HID2])
        b2_high = sb("b2_high", [1, HID2], fp32r)
        b2_low = sb("b2_low", [1, HID2], fp32r)
        ones_row = sb("ones_row", [1, 128], fp32r)
        ones = sb("ones", [128, 128])
        ident = sb("ident", [128, 128])

        last_bank_ps = pb("last_bank_ps", [128, PER_BANK, TILE])
        h2_ps = pb("h2_ps", [128, 512])
        gram_ps = [pb(f"gram_ps{i}", [128, 2, 512]) for i in range(2)]
        pairs_ps = pb("pairs_ps", [128, 2, 512])
        early_gram_ps = [gram_ps[0][:, c, :].rearrange("p (n b) -> p n b", n=PER_BANK) for c in range(2)]
        early_pairs_ps = [pairs_ps[:, c, :].rearrange("p (n b) -> p n b", n=PER_BANK) for c in range(2)]
        bank_ps = [early_pairs_ps[0], early_pairs_ps[1], early_gram_ps[0], early_gram_ps[1], last_bank_ps[:, :, :]]
        assert ROW_BANKS <= len(bank_ps)
        h1_ps = gram_ps[1][:, :, 0:H1 * TILE].rearrange("p c (j b) -> p c j b", b=TILE)
        dense_ps = gram_ps[0][:, 0, :]
        lookup_ps = [gram_ps[1][:, c, :] for c in range(2)]

        ids_loaded = sem("ids_loaded")
        lookup_ids_loaded = [sem(f"lookup_ids_loaded{j}") for j in range(LOOKUPS)]
        table_loaded = [sem(f"table_loaded{i}") for i in range(TABLE_BUFFERS)]
        row_number_i_set = sem("row_number_i_set")
        row_number_set = sem("row_number_set")
        minus_row_number_set = sem("minus_row_number_set")
        table_high_split = sem("table_high_split")
        table_low_split = sem("table_low_split")
        dve_one_hot_set = sem("dve_one_hot_set")
        act_one_hot_set = sem("act_one_hot_set")
        distance_set = sem("distance_set")
        looked_up = sem("looked_up")
        lookup_copied = sem("lookup_copied")
        dense_loaded = sem("dense_loaded")
        weights_loaded = sem("weights_loaded")
        ones_set = sem("ones_set")
        ident_set = sem("ident_set")
        w_dense_summed = sem("w_dense_summed")
        dense_transposed = sem("dense_transposed")
        dense_copied = sem("dense_copied")
        gathered = [[sem(f"gathered{place}_{bank}") for bank in range(ROW_BANKS)] for place in range(PLACES)]
        bank_transposed = sem("bank_transposed")
        act_bank_copied = sem("act_bank_copied")
        dve_bank_copied = sem("dve_bank_copied")
        resident_placed = sem("resident_placed")
        chunk_computed = sem("chunk_computed")
        act_diag_copied = sem("act_diag_copied")
        dve_diag_copied = sem("dve_diag_copied")
        gram_turned = sem("gram_turned")
        rows_repeated = sem("rows_repeated")
        act_pairs_packed = sem("act_pairs_packed")
        dve_pairs_packed = sem("dve_pairs_packed")
        pairs_turned = sem("pairs_turned")
        act_pairs_copied = sem("act_pairs_copied")
        dve_pairs_copied = sem("dve_pairs_copied")
        h1_computed = sem("h1_computed")
        act_h1_rectified = sem("act_h1_rectified")
        dve_h1_rectified = sem("dve_h1_rectified")
        b2_high_set = sem("b2_high_set")
        b2_split = sem("b2_split")
        h2_computed = sem("h2_computed")
        scored = sem("scored")
        out_written = sem("out_written")
        WEIGHT_LOADS = 16 * 6

        def slots_of(bank):
            return range(bank * PER_BANK, min((bank + 1) * PER_BANK, GATHERS))

        def tile_columns(t):
            return bass.ds(t * TILE, TILE)

        def by_slot(first, count):
            return feats[:, :, :, first:first + count].rearrange("p i s n -> p n s i")

        def samples_apart(view):
            return view.rearrange("p n (s i) -> p n s i", s=QUAD)

        def copy_bank(engine_copy, bank):
            n = len(slots_of(bank))
            return engine_copy(by_slot(bank * PER_BANK, n), samples_apart(bank_ps[bank][:, 0:n, :]))

        pairs_flat = pairs[:, :, :].rearrange("p k f -> p (k f)")

        def pair_view(first_f, count):
            base = gram_by_sample[:, 1 + first_f, first_f:first_f + 1]
            return bass.AP(base.tensor, base.offset, [list(base.ap[0]), [SLOTS, DIAGS], [SLOTS + 1, count]])

        def load_lookup_ids(engine, j):
            engine.dma_start(lookup_ids[:, j, :], ids_looked_up[j * BATCH:(j + 1) * BATCH].partition_broadcast(128)
                             ).then_inc(lookup_ids_loaded[j], 16)

        block = ctx.enter_context(nc.Block())

        @block.sync
        def _(sp):
            sp.dma_start(ids_sb[:, 0:TILES * GATHERS].rearrange("p (t f) -> p t f", t=TILES),
                         ids_gathered.rearrange("(t p) f -> p t f", p=TILE)).then_inc(ids_loaded, 16)
            def load_table(j):
                rows_first = 112 * LOOKUP_CHUNKS
                sp.dma_start(table[j % TABLE_BUFFERS][0:112, :],
                             lookup_tables[j][0:rows_first, :].rearrange("(p c) d -> p (c d)", c=LOOKUP_CHUNKS)
                             ).then_inc(table_loaded[j % TABLE_BUFFERS], 16)
                sp.dma_start(table[j % TABLE_BUFFERS][112:LOOKUP_PARTS, :],
                             lookup_tables[j][rows_first:, :].rearrange("(p c) d -> p (c d)", c=LOOKUP_CHUNKS)
                             ).then_inc(table_loaded[j % TABLE_BUFFERS], 16)

            load_table(0)
            sp.dma_start(dense_rows[:, :, :], dense.rearrange("(t p) d -> p t d", p=TILE)).then_inc(dense_loaded, 16)
            load_lookup_ids(sp, 1)
            for j in range(1, LOOKUPS):
                if j >= TABLE_BUFFERS:
                    sp.wait_ge(table_low_split, j - TABLE_BUFFERS + 1)
                load_table(j)
                if j + 1 < LOOKUPS:
                    load_lookup_ids(sp, j + 1)
            sp.dma_start(w_pairs_sb[:, :, :],
                         w_pairs.rearrange("(t p) n -> p t n", p=PAIR_ROWS)).then_inc(weights_loaded, 16)
            sp.dma_start(w2_sb[:, :, :], w2.rearrange("(j p) n -> p j n", p=128)).then_inc(weights_loaded, 16)
            sp.dma_start(w_dense2_sb[:, :, :], w_dense.rearrange("(c p) n -> p c n", c=2)).then_inc(weights_loaded, 16)
            with nc.allow_non_contiguous_dma(reason="bias, one value per partition"):
                sp.dma_start(b1_sb[:, :], b1.rearrange("(j p) -> p j", p=128)).then_inc(weights_loaded, 16)
            sp.dma_start(b2_sb[:, :], b2.rearrange("(o n) -> o n", o=1)).then_inc(weights_loaded, 16)
            sp.dma_start(w3_sb[:, :],
                         w3.rearrange("n o -> (n o)").partition_broadcast(128)).then_inc(weights_loaded, 16)
            for first, end in ((0, TILES - 1), (TILES - 1, TILES)):
                sp.wait_ge(scored, end)
                with nc.allow_non_contiguous_dma(reason="results, one value per partition and tile"):
                    sp.dma_start(out[:, first:end], y[:, first:end]).then_inc(out_written, 16)
            sp.wait_ge(out_written, 2 * 16)

        @block.gpsimd
        def _(pool):
            nc.gpsimd.iota(row_number_i[:, :], pattern=[[1, LOOKUP_CHUNKS]], base=0,
                           channel_multiplier=LOOKUP_CHUNKS).then_inc(row_number_i_set, 1)
            nc.gpsimd.memset(ones[:, :], 1.0).then_inc(ones_set, 1)
            pool.wait_ge(ones_set, 1)
            nc.gpsimd.affine_select(out=ident[:, :], in_=ones[:, :], compare_op=ALU.is_equal, fill=0.0, base=0,
                                    pattern=[[-1, 128]], channel_multiplier=1).then_inc(ident_set, 1)

            pool.wait_ge(ids_loaded, 16)
            for t in range(TILES):
                place = min(t, PLACES - 1)
                for bank in range(ROW_BANKS):
                    if t >= PLACES:
                        pool.wait_ge(bank_transposed, (t - 1) * ROW_BANKS + bank + 1)
                        pool.nop(nofuse=True)
                    for slot in slots_of(bank):
                        ids_column = t * GATHERS + slot
                        nc.gpsimd.indirect_dma_start(
                            out=rows[place][:, slot, :], out_offset=None, in_=gathered_tables[slot],
                            in_offset=bass.IndirectOffsetOnAxis(ap=ids_sb[:, ids_column:ids_column + 1], axis=0),
                        ).then_inc(gathered[place][bank], 16)

        @block.tensor
        def _(pe):
            def look_up(j):
                if j >= 2:
                    pe.wait_ge(lookup_copied, j - 1)
                for chunks in (range(DVE_CHUNKS[j]), range(DVE_CHUNKS[j], LOOKUP_CHUNKS)):
                    pe.wait_ge(table_high_split, j + 1)
                    for c in chunks:
                        if c < DVE_CHUNKS[j]:
                            pe.wait_ge(dve_one_hot_set, DVE_CHUNKS_BEFORE[j] + c + 1)
                        else:
                            pe.wait_ge(act_one_hot_set, ACT_CHUNKS_BEFORE[j] + c - DVE_CHUNKS[j] + 1)
                        nc.tensor.matmul(lookup_ps[j % 2], table_high[j % SPLIT_BUFFERS][:, c * DIM:(c + 1) * DIM],
                                         one_hot[j % 2][c][:, :], start=(c == 0), stop=False)
                    pe.wait_ge(table_low_split, j + 1)
                    for c in chunks:
                        last = nc.tensor.matmul(lookup_ps[j % 2],
                                                table_low[j % SPLIT_BUFFERS][:, c * DIM:(c + 1) * DIM],
                                                one_hot[j % 2][c][:, :], start=False, stop=(c == LOOKUP_CHUNKS - 1))
                last.then_inc(looked_up, 1)

            def transpose_bank(t, place, bank):
                if place == 0 and bank == 2:
                    pe.wait_ge(dense_copied, 1)
                if bank in (2, 3) and place > 0:
                    pe.wait_ge(act_diag_copied, t * CHUNKS - 2)
                    pe.wait_ge(dve_diag_copied, t * CHUNKS - 2)
                tiles_here = t - (PLACES - 2) if place == PLACES - 1 else 1
                pe.wait_ge(gathered[place][bank], tiles_here * (16 * len(slots_of(bank))))
                for slot in slots_of(bank):
                    last = nc.tensor.transpose(bank_ps[bank][:, slot % PER_BANK, :], rows[place][:, slot, :],
                                               ident[:, :])
                last.then_inc(bank_transposed, 1)

            def second_layer(t):
                for half, rectified in enumerate((act_h1_rectified, dve_h1_rectified)):
                    pe.wait_ge(rectified, t + 1)
                    for k in range(half * H1, (half + 1) * H1):
                        last = nc.tensor.matmul(h2_ps[:, 0:HID2], h1_t[:, k, :], w2_sb[:, k, :], start=False,
                                                stop=(k == J1 - 1))
                last.then_inc(h2_computed, 1)

            def second_layer_bias():
                pe.wait_ge(b2_split, 1)
                nc.tensor.matmul(h2_ps[:, 0:HID2], ones_row[:, :], b2_high[:, :], start=True, stop=False)
                nc.tensor.matmul(h2_ps[:, 0:HID2], ones_row[:, :], b2_low[:, :], start=False, stop=False)

            def first_layer_of_dense(t, half):
                pe.wait_ge(weights_loaded, WEIGHT_LOADS)
                pe.wait_ge(w_dense_summed, 1)
                for j in range(half * H1, (half + 1) * H1):
                    nc.tensor.matmul(h1_ps[:, j // H1, j % H1, :], w_dense2_sb[:, 0, j * 128:(j + 1) * 128],
                                     resident[:, 0, tile_columns(t)], start=(j % H1 == 0), stop=False,
                                     skip_group_check=True)

            def interact_and_classify(t, led, followed):
                pe.wait_ge(act_bank_copied, t * len(ACT_BANKS) + len(ACT_BANKS))
                pe.wait_ge(dve_bank_copied, t * len(DVE_BANKS) + len(DVE_BANKS))
                pe.wait_ge(resident_placed, t + 1)
                for chunk in range(CHUNKS):
                    if chunk == 1 and not led:
                        pe.wait_ge(lookup_copied, LOOKUPS)
                    if chunk == 1 and led:
                        pe.wait_ge(act_h1_rectified, t)
                        pe.wait_ge(dve_h1_rectified, t)
                    if chunk >= 2:
                        pe.wait_ge(act_diag_copied, t * CHUNKS + min(chunk - 1, 2))
                        pe.wait_ge(dve_diag_copied, t * CHUNKS + min(chunk - 1, 2))
                    for bank in CHUNK_BANKS[chunk]:
                        for at in range(PER_BANK):
                            i = bank * PER_BANK + at
                            last = nc.tensor.matmul(
                                gram_ps[bank // 2 % 2][0:GRAM_ROWS, bank % 2,
                                                       at * GRAM_COLS:(at + 1) * GRAM_COLS].rearrange(
                                    "p (s g) -> p s g", s=QUAD),
                                feats[:, i, :, :].rearrange("p s f -> p (s f)")[:, 0:GRAM_ROWS],
                                feats[:, i, :, 0:FEATS], start=True, stop=True)
                    last.then_inc(chunk_computed, 1)
                early_banks = EARLY_BANKS if led else ROW_BANKS - 1
                late_banks = LATE_BANKS if led else ROW_BANKS
                if followed:
                    for bank in range(early_banks):
                        transpose_bank(t + 1, 2 if led else 1, bank)
                if led:
                    second_layer(t - 1)
                pe.wait_ge(act_diag_copied, t * CHUNKS + CHUNKS)
                pe.wait_ge(dve_diag_copied, t * CHUNKS + CHUNKS)
                first_layer_of_dense(t, 0)
                if not led:
                    first_layer_of_dense(t, 1)
                pe.wait_ge(act_pairs_packed, t + 1)
                pe.wait_ge(dve_pairs_packed, t + 1)
                if followed:
                    pe.wait_ge(act_bank_copied, t * len(ACT_BANKS) + (len(ACT_BANKS) + EARLY_BANKS))
                for k in range(PAIR_TILES):
                    last = nc.tensor.transpose(pairs_ps[0:PAIR_ROWS, k // 2, (k % 2) * TILE:(k % 2 + 1) * TILE],
                                               pairs_flat[:, k * PAIR_ROWS:(k + 1) * PAIR_ROWS], ident[:, :])
                    if k % 2 == 1 or k == PAIR_TILES - 1:
                        last.then_inc(pairs_turned, 1)
                if led:
                    first_layer_of_dense(t, 1)
                    pe.wait_ge(scored, t)
                second_layer_bias()
                if followed:
                    for bank in range(early_banks, late_banks):
                        transpose_bank(t + 1, 2 if led else 1, bank)
                pe.wait_ge(act_pairs_copied, t + 1)
                for half in range(2):
                    for k in range(PAIR_TILES):
                        if k == PAIR_TILES - 1 and half == 0:
                            pe.wait_ge(dve_pairs_copied, t + 1)
                        if k == PAIR_TILES - 1 and half == 1 and led and followed:
                            transpose_bank(t + 1, 2, ROW_BANKS - 1)
                        for j in range(half * H1, (half + 1) * H1):
                            last = nc.tensor.matmul(h1_ps[:, half, j % H1, :],
                                                    w_pairs_sb[:, k, j * 128:(j + 1) * 128], pairs_t[:, k, :],
                                                    start=False, stop=(k == PAIR_TILES - 1), skip_group_check=True)
                    last.then_inc(h1_computed, 1)
                    if half == 0 and led and followed:
                        for bank in range(late_banks, ROW_BANKS - 1):
                            transpose_bank(t + 1, 2 if led else 1, bank)

            pe.wait_ge(ones_set, 1)
            for _ in range(WARM_UP):
                nc.tensor.matmul(h2_ps[0:1, 0:128], ones[:, 0:1], ones[:, :], start=True, stop=True)
            pe.wait_ge(ident_set, 1)
            pe.wait_ge(dense_loaded, 16)
            for t in range(TILES):
                last = nc.tensor.transpose(dense_ps[:, t * TILE:(t + 1) * TILE], dense_rows[:, t, :], ident[:, :])
            last.then_inc(dense_transposed, 1)
            for j in range(LOOKUPS):
                look_up(j)
                if j < ROW_BANKS:
                    transpose_bank(0, 0, j)
            for bank in range(LOOKUPS, ROW_BANKS):
                transpose_bank(0, 0, bank)
            interact_and_classify(0, False, True)
            with pe.Fori(1, TILES - 1) as t:
                interact_and_classify(t, True, True)
            interact_and_classify(TILES - 1, True, False)
            second_layer(TILES - 1)

        def copy_diagonal(engine_copy, chunk, s):
            banks = CHUNK_BANKS[chunk]
            first, n = banks[0], len(banks)
            return engine_copy(
                gram[SLOTS * s:SLOTS * s + FEATS, first * PER_BANK:(first + n) * PER_BANK, :].rearrange(
                    "p (c q) g -> p c q g", c=n),
                gram_ps[first // 2 % 2][SLOTS * s:SLOTS * s + FEATS, first % 2:first % 2 + n,
                                        0:PER_BANK * GRAM_COLS].rearrange(
                    "p c (q s g) -> p c q s g", q=PER_BANK, s=QUAD)[:, :, :, s, :])

        ACT_SAMPLES = 2

        @block.scalar
        def _(act):
            def split_table_high(j):
                act.wait_ge(table_loaded[j % TABLE_BUFFERS], (j // TABLE_BUFFERS + 1) * 32)
                if j >= SPLIT_BUFFERS:
                    act.wait_ge(looked_up, j - SPLIT_BUFFERS + 1)
                nc.scalar.copy(table_high[j % SPLIT_BUFFERS][:, :], table[j % TABLE_BUFFERS][:, :]
                               ).then_inc(table_high_split, 1)

            def copy_lookup(j):
                act.wait_ge(looked_up, j + 1)
                if j == LOOKUPS - 1:
                    act.wait_ge(resident_placed, 1)
                nc.scalar.copy(resident[:, 1 + j, :], lookup_ps[j % 2]).then_inc(lookup_copied, 1)

            def copy_transposed_bank(t, bank):
                act.wait_ge(bank_transposed, t * ROW_BANKS + (bank + 1))
                copy_bank(nc.scalar.copy, bank).then_inc(act_bank_copied, 1)

            def set_distance(j):
                if j == 0:
                    act.wait_ge(minus_row_number_set, 1)
                act.wait_ge(lookup_ids_loaded[j], 16)
                if j > 0:
                    act.wait_ge(act_one_hot_set, ACT_CHUNKS_BEFORE[j])
                for n in range(ACT_CHUNKS[j]):
                    c = DVE_CHUNKS[j] + n
                    nc.scalar.activation(distance[n][:, :], lookup_ids[0:LOOKUP_PARTS, j, :], ACT.Abs,
                                         bias=minus_row_number[0:LOOKUP_PARTS, c:c + 1]).then_inc(distance_set, 1)

            def set_one_hot(j):
                if j >= 2:
                    act.wait_ge(looked_up, j - 1)
                for n in range(ACT_CHUNKS[j]):
                    act.wait_ge(distance_set, ACT_CHUNKS_BEFORE[j] + n + 1)
                    nc.scalar.activation(one_hot[j % 2][DVE_CHUNKS[j] + n][:, :], distance[n][:, :], ACT.Relu, bias=1.0,
                                         scale=-1.0).then_inc(act_one_hot_set, 1)

            def interact_and_classify(t, led, followed):
                for chunk in range(CHUNKS):
                    act.wait_ge(chunk_computed, t * CHUNKS + (chunk + 1))
                    for s in range(ACT_SAMPLES):
                        last = copy_diagonal(nc.scalar.copy, chunk, s)
                    last.then_inc(act_diag_copied, 1)
                if followed:
                    copy_transposed_bank(t + 1, 0)
                act.wait_ge(gram_turned, t * 2 + 1)
                nc.scalar.copy(gram_by_sample[:, FEATS:FEATS + DIAGS, 0:FEATS], gram_by_sample[:, 0:DIAGS, 0:FEATS]
                               ).then_inc(rows_repeated, 1)
                act.wait_ge(gram_turned, t * 2 + 2)
                nc.scalar.copy(pairs[:, :, 0:UNWRAPPED], pair_view(0, UNWRAPPED)).then_inc(act_pairs_packed, 1)
                if followed:
                    copy_transposed_bank(t + 1, 1)
                act.wait_ge(pairs_turned, t * 2 + 1)
                nc.scalar.copy(pairs_t[:, 0:2, :].rearrange("p k b -> p (k b)"),
                               pairs_ps[0:PAIR_ROWS, 0, 0:2 * TILE]).then_inc(act_pairs_copied, 1)
                if followed and not led:
                    for bank in ACT_BANKS[EARLY_BANKS:]:
                        copy_transposed_bank(t + 1, bank)
                act.wait_ge(weights_loaded, WEIGHT_LOADS)
                act.wait_ge(h1_computed, t * 2 + 1)
                for j in range(H1):
                    last = nc.scalar.activation(h1_t[:, j, :], h1_ps[:, 0, j, :], ACT.Relu, bias=b1_sb[:, j:j + 1])
                last.then_inc(act_h1_rectified, 1)
                if followed and led:
                    for bank in ACT_BANKS[EARLY_BANKS:]:
                        copy_transposed_bank(t + 1, bank)

            load_lookup_ids(act, 0)
            act.wait_ge(row_number_i_set, 1)
            nc.scalar.activation(row_number[:, :], row_number_i[:, :], ACT.Abs).then_inc(row_number_set, 1)
            set_distance(0)
            split_table_high(0)
            set_one_hot(0)
            split_table_high(1)
            for j in range(LOOKUPS):
                if j + 1 < LOOKUPS:
                    set_distance(j + 1)
                    set_one_hot(j + 1)
                if j == 0:
                    act.wait_ge(dense_transposed, 1)
                    nc.scalar.copy(resident[:, 0, :], dense_ps).then_inc(dense_copied, 1)
                if j + 2 < LOOKUPS:
                    split_table_high(j + 2)
                copy_lookup(j)
                if j in ACT_BANKS:
                    copy_transposed_bank(0, j)
            interact_and_classify(0, False, True)
            with act.Fori(1, TILES - 1) as t:
                interact_and_classify(t, True, True)
            interact_and_classify(TILES - 1, True, False)

        @block.vector
        def _(dve):
            def set_one_hot(j):
                dve.wait_ge(lookup_ids_loaded[j], 16)
                if j >= 2:
                    dve.wait_ge(looked_up, j - 1)
                for c in range(DVE_CHUNKS[j]):
                    nc.vector.tensor_scalar(one_hot[j % 2][c][:, :], lookup_ids[0:LOOKUP_PARTS, j, :],
                                            row_number[0:LOOKUP_PARTS, c:c + 1], None,
                                            ALU.is_equal).then_inc(dve_one_hot_set, 1)

            def split_table_low(j):
                dve.wait_ge(table_high_split, j + 1)
                nc.vector.tensor_tensor(table_low[j % SPLIT_BUFFERS][:, :], table[j % TABLE_BUFFERS][:, :],
                                        table_high[j % SPLIT_BUFFERS][:, :], ALU.subtract).then_inc(table_low_split, 1)

            def copy_transposed_bank(t, bank):
                dve.wait_ge(bank_transposed, t * ROW_BANKS + (bank + 1))
                copy_bank(nc.vector.tensor_copy, bank).then_inc(dve_bank_copied, 1)

            def place_resident(t):
                nc.vector.tensor_copy(by_slot(GATHERS, RESIDENT),
                                      samples_apart(resident[:, :, tile_columns(t)])).then_inc(resident_placed, 1)

            def score(t):
                dve.wait_ge(h2_computed, t + 1)
                nc.vector.scalar_tensor_tensor(out=weighted[:, :], in0=h2_ps[:, 0:HID2], scalar=0.0,
                                               in1=w3_sb[:, :], op0=ALU.max, op1=ALU.mult,
                                               accum_out=y[:, bass.ds(t, 1)]).then_inc(scored, 1)

            def interact_and_classify(t, led, followed):
                for chunk in range(CHUNKS):
                    dve.wait_ge(chunk_computed, t * CHUNKS + (chunk + 1))
                    for s in range(ACT_SAMPLES, QUAD):
                        last = copy_diagonal(nc.vector.tensor_copy, chunk, s)
                    last.then_inc(dve_diag_copied, 1)
                dve.wait_ge(act_diag_copied, (t + 1) * CHUNKS)
                dve.wait_ge(dve_diag_copied, (t + 1) * CHUNKS)
                for first, end in ((0, DIAGS), (DIAGS, FEATS)):
                    nc.vector.transpose(gram_by_sample[:, first:end, :],
                                        gram[:, :, first:end].rearrange("p i g -> p g i")).then_inc(gram_turned, 1)
                dve.wait_ge(gram_turned, t * 2 + 2)
                dve.wait_ge(rows_repeated, t + 1)
                nc.vector.tensor_copy(pairs[:, :, UNWRAPPED:FEATS],
                                      pair_view(UNWRAPPED, FEATS - UNWRAPPED)).then_inc(dve_pairs_packed, 1)
                if led:
                    score(t - 1)
                dve.wait_ge(pairs_turned, t * 2 + 2)
                nc.vector.tensor_copy(pairs_t[:, 2, :], pairs_ps[0:PAIR_ROWS, 1, 0:TILE]).then_inc(dve_pairs_copied, 1)
                if followed:
                    place_resident(t + 1)
                    for bank in DVE_BANKS:
                        copy_transposed_bank(t + 1, bank)
                dve.wait_ge(h1_computed, t * 2 + 2)
                for j in range(H1, J1):
                    last = nc.vector.tensor_scalar(h1_t[:, j, :], h1_ps[:, 1, j - H1, :], b1_sb[:, j:j + 1], 0.0,
                                                   ALU.add, ALU.max)
                last.then_inc(dve_h1_rectified, 1)

            nc.vector.memset(gram[:, :, :], 0.0)
            nc.vector.memset(feats[:, :, :, FEATS:SLOTS], 0.0)
            dve.wait_ge(row_number_i_set, 1)
            nc.vector.tensor_scalar(minus_row_number[:, :], row_number_i[:, :], -1.0, None,
                                    ALU.mult).then_inc(minus_row_number_set, 1)
            dve.wait_ge(row_number_set, 1)
            dve.wait_ge(ones_set, 1)
            set_one_hot(0)
            split_table_low(0)
            for j in range(LOOKUPS):
                if j + 1 < LOOKUPS:
                    set_one_hot(j + 1)
                    split_table_low(j + 1)
                if j in DVE_BANKS:
                    copy_transposed_bank(0, j)
            dve.wait_ge(dense_copied, 1)
            dve.wait_ge(lookup_copied, LOOKUPS - 1)
            nc.vector.tensor_copy(by_slot(GATHERS, RESIDENT - 1), samples_apart(resident[:, 0:RESIDENT - 1, 0:TILE]))
            dve.wait_ge(looked_up, LOOKUPS)
            nc.vector.tensor_copy(by_slot(GATHERS + RESIDENT - 1, 1),
                                  lookup_ps[(LOOKUPS - 1) % 2][:, 0:TILE].rearrange("p (n s i) -> p n s i", n=1, s=QUAD)
                                  ).then_inc(resident_placed, 1)
            dve.wait_ge(lookup_copied, LOOKUPS)
            dve.wait_ge(weights_loaded, WEIGHT_LOADS)
            nc.vector.tensor_tensor(w_dense2_sb[:, 0, :], w_dense2_sb[:, 0, :], w_dense2_sb[:, 1, :],
                                    ALU.add).then_inc(w_dense_summed, 1)
            nc.vector.tensor_copy(ones_row[:, :], ones[0:1, :])
            nc.vector.tensor_copy(b2_high[:, :], b2_sb[:, :]).then_inc(b2_high_set, 1)
            dve.wait_ge(b2_high_set, 1)
            nc.vector.tensor_tensor(b2_low[:, :], b2_sb[:, :], b2_high[:, :], ALU.subtract).then_inc(b2_split, 1)
            interact_and_classify(0, False, True)
            with dve.Fori(1, TILES - 1) as t:
                interact_and_classify(t, True, True)
            interact_and_classify(TILES - 1, True, False)
            score(TILES - 1)


def kernel(**inputs):
    import concourse.bacc as bacc
    from concourse.bass_utils import run_bass_kernel_spmd

    ids = np.asarray(inputs["ids"])
    w1 = np.asarray(inputs["W_top1"])
    arrays = {
        "dense": np.ascontiguousarray(inputs["r_dense_features"]),
        "ids_gathered": np.ascontiguousarray(ids[:, GATHERED]),
        "ids_looked_up": np.ascontiguousarray(ids[:, LOOKED_UP].T.reshape(-1)),
        "w_pairs": np.ascontiguousarray(w1[pair_row_order()]),
        "w_dense": np.ascontiguousarray(np.concatenate([w1[:DIM], w1[-DIM:]])),
    }
    tables = [f"tbl_{f}" for f in range(FIELDS)]
    for name in tables + ["b_top1", "W_top2", "b_top2", "W_top3"]:
        arrays[name] = np.ascontiguousarray(inputs[name])

    nc = bacc.Bacc("TRN2", target_bir_lowering=False, num_devices=1)
    ap = {name: nc.dram_tensor("in_" + name, a.shape, mybir.dt.from_np(a.dtype), kind="ExternalInput").ap()
          for name, a in arrays.items()}
    out = nc.dram_tensor("out_y", (BATCH, 1), mybir.dt.float32, kind="ExternalOutput").ap()
    dlrm_tower(nc, ap["dense"], ap["ids_gathered"], ap["ids_looked_up"], [ap[tables[f]] for f in GATHERED],
               [ap[tables[f]] for f in LOOKED_UP], ap["w_pairs"], ap["w_dense"], ap["b_top1"], ap["W_top2"],
               ap["b_top2"], ap["W_top3"], out.rearrange("(t p) o -> p (t o)", p=TILE))
    r = run_bass_kernel_spmd(nc, [{"in_" + name: a for name, a in arrays.items()}], core_ids=[0])
    return r.results[0]["out_y"]
```
